# Optimizing a Trainium2 kernel written in Bass

```python
import numpy as np
import jax
import jax.numpy as jnp

def _softmax(x, axis=-1):
    return jax.nn.softmax(x, axis=axis)
def _gelu(x):
    return jax.nn.gelu(x, approximate=True)
def _silu(x):
    return jax.nn.silu(x)
def _sigmoid(x):
    return jax.nn.sigmoid(x)
def _layernorm(x, axis=-1, eps=1e-5):
    m = jnp.mean(x, axis=axis, keepdims=True)
    v = jnp.var(x, axis=axis, keepdims=True)
    return (x - m) / jnp.sqrt(v + eps)
def _scatter_add(tgt, idx, src, axis=0):
    return tgt.at[idx].add(src)
def _segment_sum(src, seg, n):
    return jax.ops.segment_sum(src, seg, n)

kernel_name = 'mk_conv_preact_d1_conv_nchw384_be76ce'

def setup_inputs(seed: int = 0):
    np.random.seed(seed)
    _w = jnp.asarray
    def _rec_inputs():
        import jax
        import jax.numpy as jnp
        _gk = jax.random.key(seed)
        x = -4.65e-05 + 0.9999 * jax.random.normal(jax.random.fold_in(_gk, 1), (2, 384, 256, 256), jnp.float32)
        return x
    x = _rec_inputs()
    def _L0_conv_setup():
        import jax, jax.numpy as jnp
        import numpy as np
        B, DIM, H, W = (2, 384, 256, 256)
        HID = DIM * 1
        P = 8
        key = jax.random.key(seed)
        k0, k1, k2, k3, k4 = jax.random.split(key, 5)
        x = jax.random.normal(k0, (B, DIM, H, W), jnp.float32)
        fft_filter = jax.random.normal(k1, (HID, P, P // 2 + 1), jnp.float32)
        w_in = jax.random.normal(k2, (HID, DIM), jnp.float32) * (1.0 / np.sqrt(DIM))
        w_dw = jax.random.normal(k3, (HID, 1, 3, 3), jnp.float32) * (1.0 / 3.0)
        w_out = jax.random.normal(k4, (DIM, HID // 2), jnp.float32) * (1.0 / np.sqrt(HID // 2))
        return {'x': x, 'fft_filter': fft_filter, 'w_in': w_in, 'w_dw': w_dw, 'w_out': w_out}
    _L0_conv_all = _L0_conv_setup()
    _L0_conv_in = {k: v for k, v in _L0_conv_all.items() if k in ('fft_filter', 'w_in', 'w_dw', 'w_out', )}
    del _L0_conv_all

    return {
        "x": x,
        "L0_conv_fft_filter": _L0_conv_in["fft_filter"],
        "L0_conv_w_in": _L0_conv_in["w_in"],
        "L0_conv_w_dw": _L0_conv_in["w_dw"],
        "L0_conv_w_out": _L0_conv_in["w_out"],
    }

def reference(x, L0_conv_fft_filter, L0_conv_w_in, L0_conv_w_dw, L0_conv_w_out):
    import jax
    import jax.numpy as jnp
    def _L0_conv_ref(x, fft_filter, w_in, w_dw, w_out):
        import jax, jax.numpy as jnp
        import numpy as np
        B, DIM, H, W = (2, 384, 256, 256)
        HID = DIM * 1
        P = 8
        b, c, h, w = x.shape
        hid = w_in.shape[0]
        hb, wb = (h // P, w // P)
        t = jnp.einsum('bchw,oc->bohw', x, w_in)
        tp = t.reshape(b, hid, hb, P, wb, P)
        tf = jnp.fft.rfft2(tp, axes=(3, 5))
        tf = tf * fft_filter[None, :, None, :, None, :]
        tp = jnp.fft.irfft2(tf, s=(P, P), axes=(3, 5))
        t = tp.reshape(b, hid, h, w)
        t = jax.lax.conv_general_dilated(t, w_dw, window_strides=(1, 1), padding='SAME', feature_group_count=hid, dimension_numbers=('NCHW', 'OIHW', 'NCHW'))
        x1, x2 = (t[:, :hid // 2], t[:, hid // 2:])
        g = jax.nn.gelu(x1, approximate=False) * x2
        return jnp.einsum('bchw,oc->bohw', g, w_out)

    def _gn(v, G=32, eps=1e-5):
        B_, C_, H_, W_ = v.shape
        g = v.reshape(B_, G, C_ // G, H_, W_)
        m = jnp.mean(g, axis=(2, 3, 4), keepdims=True)
        s = jnp.var(g, axis=(2, 3, 4), keepdims=True)
        return ((g - m) / jnp.sqrt(s + eps)).reshape(v.shape)

    def _ln_c(v, eps=1e-6):
        m = jnp.mean(v, axis=1, keepdims=True)
        s = jnp.var(v, axis=1, keepdims=True)
        return (v - m) / jnp.sqrt(s + eps)

    def _ln_t(v, eps=1e-5):
        m = jnp.mean(v, axis=-1, keepdims=True)
        s = jnp.var(v, axis=-1, keepdims=True)
        return (v - m) / jnp.sqrt(s + eps)

    def _to_tokens(v):
        B_, C_, H_, W_ = v.shape
        return v.reshape(B_, C_, H_ * W_).transpose(0, 2, 1)
    def _from_tokens(t, like):
        B_, C_, H_, W_ = like.shape
        return t.transpose(0, 2, 1).reshape(B_, C_, H_, W_)

    x = x + _L0_conv_ref(_gn(x), L0_conv_fft_filter, L0_conv_w_in, L0_conv_w_dw, L0_conv_w_out)
    return x


_drawn_inputs = setup_inputs


def setup_inputs(seed=0):
    import zlib

    import numpy as np

    out = dict(_drawn_inputs(seed))
    spreads = {}
    factors = {}
    for name, (base, spread) in spreads.items():
        noise = np.random.default_rng([zlib.crc32(name.encode()), seed]).standard_normal(out[name].shape)
        drawn = base * np.exp(spread * noise) if base else spread * noise
        out[name] = jnp.asarray(drawn.astype(out[name].dtype))
    for name, factor in factors.items():
        out[name] = (out[name] * factor).astype(out[name].dtype)
    return out
```

```python
from contextlib import ExitStack

import concourse.bass as bass
from concourse import mybir

F32 = mybir.dt.float32
ALU = mybir.AluOpType
ACT = mybir.ActivationFunctionType

P = 128
EDGE = 8
NB, CH, H, W = 2, 384, 256, 256
KT = CH // P
GROUPS = 32
CPG = CH // GROUPS
EPS = 1e-5
STRIPS = H // EDGE
NS = NB * STRIPS
GC = 64
NG = W // GC
PC = 16
NPAIR = GC // PC
HC = W // 2
TW = W + 2
WIN = EDGE * W
BN = 512
CHUNK = WIN
NCHUNK = H * W // CHUNK
RING = 4
HID2 = CH // 2
LO = HID2 - P

ACC0, ACC1, ACC2, NACC = 0, (1, 2), (3, 4), 5


def acc_of(tile, w):
    return ACC0 if tile == 0 else (ACC1, ACC2)[tile - 1][w % 2]


def begins(w):
    return w < NS and w % STRIPS == 0


def firsts(w):
    return (w + STRIPS - 1) // STRIPS if w < NS else NB


def n_taps(tile, w):
    per = 8 if tile else 9
    edge_taps = 5 if tile else 6
    return edge_taps if w == NS else per + (edge_taps if begins(w) else 0)


def taps_before(tile, w, w0):
    if w0 == NS + 1:
        return taps_before(tile, NS, NS) + n_taps(tile, NS)
    return w * n_taps(tile, 1) + firsts(w0) * (n_taps(tile, 0) - n_taps(tile, 1))


def stores_before(w, w0):
    return w + sum(1 for b in range(1, NB) if w0 > b * STRIPS)


def conv_kernel(nc, x, w_in, w_out, w_dw, filt, dft, dft_t, select, group_mean, out):
    xc = x.rearrange("b (k p) h w -> (b k) p (h w)", p=P)
    orow = out.rearrange("b (k p) h w -> (b k) p h w", p=P)
    xr = x.rearrange("b (k p) h w -> (b k) p h w", p=P)

    with ExitStack() as ctx:
        def sb(name, shape, dt=F32):
            return ctx.enter_context(nc.sbuf_tensor(name, shape, dt))

        def sem(name):
            return ctx.enter_context(nc.semaphore(name))

        t_buf = sb("t_buf", [P, 2, KT, EDGE + 2, TW])
        edge = sb("edge", [P, KT, 2, TW])
        zrows = sb("zrows", [P, 2, TW])
        acc = sb("acc", [P, NACC, EDGE, W])
        y = sb("y", [P, KT, EDGE, W])
        xh = sb("xh", [P, 2, KT, EDGE, HC])
        xp = sb("xp", [P, 2, KT, NPAIR, EDGE * PC])
        ta = sb("ta", [P, 2, 2, CH])
        tf = sb("tf", [P, 2, 2, 2, CH])
        wi = sb("wi", [P, NB, KT, CH])
        wo = sb("wo", [P, 2, CH])
        fil = sb("fil", [P, 2, CH])
        dft_s = sb("dft_s", [P, P])
        dftt_s = sb("dftt_s", [P, P])
        taps = sb("taps", [P, KT, 10])
        beta = sb("beta", [P, NB, KT])
        mv = sb("mv", [P, NB * KT, 2])
        gst = sb("gst", [P, 10, NB * KT])
        gmean_s = y[:, 0].rearrange("p a b -> p (a b)")[:, 0:KT * CH].rearrange("p (k c) -> p k c", k=KT)
        wraw = y[:, 1].rearrange("p a b -> p (a b)")[:, 0:KT * CH].rearrange("p (k c) -> p k c", k=KT)
        yl = y[:, 2].rearrange("p a b -> p (a b)")
        NSTAT = NCHUNK * (CHUNK // BN)
        bnst = yl[:, 0:NSTAT * 6]
        sel_s = yl[0:40, 1024:1024 + P]
        filt_s = yl[0:40, 1280:1280 + CH]

        ps = ctx.enter_context(nc.psum_tensor("ps", [P, 8, 512], F32))

        set_in = sem("set_in")
        chunk_in = [sem(f"chunk_in{r}") for r in range(RING)]
        chunk_used = sem("chunk_used")
        stat_ready = sem("stat_ready")
        gs = sem("gs")
        gp = sem("gp")
        ga = sem("ga")
        wi_ready = sem("wi_ready")
        beta_ready = sem("beta_ready")
        zeroed = sem("zeroed")
        edge_ready = sem("edge_ready")
        x_in = [sem("x_in0"), sem("x_in1")]
        xp_ready = sem("xp_ready")
        a_done = sem("a_done")
        ta_ready = sem("ta_ready")
        b_done = sem("b_done")
        tf_ready = sem("tf_ready")
        d_done = sem("d_done")
        t_ready = sem("t_ready")
        halo_ready = sem("halo_ready")
        center_ready = [sem(f"center_ready{k}") for k in range(KT)]
        tap = [sem(f"tap{k}") for k in range(KT)]
        gelu_ready = sem("gelu_ready")
        g_ready = sem("g_ready")
        w_done = sem("w_done")
        y_ready = sem("y_ready")
        res_in = [sem(f"res_in{m}") for m in range(KT)]
        stored = [sem(f"stored{m}") for m in range(KT)]

        def wait(eng, s, value):
            if not isinstance(value, int) or value > 0:
                eng.wait_ge(s, value)

        def pipeline(eng, step):
            for b in range(NB):
                s0 = b * STRIPS
                for S in range(s0, s0 + 3):
                    step(S, S)
                with eng.Fori(0, STRIPS // 2 - 2) as i:
                    for u in range(s0 + 3, s0 + 5):
                        step(i * 2 + u, u)
                step(s0 + STRIPS - 1, s0 + STRIPS - 1)
            for S in range(NS, NS + 3):
                step(S, S)

        def dw_rows(w0, k):
            par = w0 % 2
            whole = (0, EDGE, lambda di, r: t_buf[:, par, k, 1 + di + r:1 + di + r + EDGE], (-1, 0, 1))
            if w0 == NS:
                return [(0, 1, lambda di, r: edge[:, k, 1 + di:2 + di], (-1, 0))]
            if begins(w0):
                return [(1, EDGE - 1, lambda di, r: t_buf[:, par, k, 2 + di:1 + di + EDGE], (-1, 0, 1)),
                        (0, 1, lambda di, r: edge[:, k, 1 + di:2 + di], (-1, 0))]
            return [whole]

        def dw_ops(w0, k):
            ops = []
            for r0, nr, source, dis in dw_rows(w0, k):
                for di in dis:
                    for dj in (-1, 0, 1):
                        ops.append((acc[:, acc_of(k, w0), r0:r0 + nr], source(di, 0)[:, :, 1 + dj:1 + dj + W],
                                    taps[:, k, (di + 1) * 3 + dj + 1:(di + 1) * 3 + dj + 2], di == 0 and dj == 0))
            return [o[:3] for o in ops if o[3]], [o[:3] for o in ops if not o[3]]

        def gelu2(w0, rows):
            return t_buf[P - LO:P, w0 % 2, 2, 0:rows, 1:1 + W]

        def y_parts(w, w0):
            b = min(w0 // STRIPS, NB - 1)
            if w0 < NS and not begins(w0):
                return [(b, (w - b * STRIPS) * EDGE - 1, 0, EDGE)]
            parts = [(b, 0, 1, EDGE - 1)] if w0 < NS else []
            return parts + [((w0 - 1) // STRIPS, H - 1, 0, 1)] * (w0 > 0)

        def win_rows(w0):
            return 1 if w0 == NS else EDGE

        block = ctx.enter_context(nc.Block())

        @block.sync
        def _(sp):
            for dst, src in ((wraw, w_in.rearrange("(k p) o -> p k o", p=P)),
                             (gmean_s, group_mean.rearrange("(k p) o -> p k o", p=P)),
                             (wo[:, 0], w_out[0:P]),
                             (wo[P - LO:P, 1], w_out[P:HID2]),
                             (dft_s[:], dft), (dftt_s[:], dft_t), (sel_s, select), (filt_s, filt),
                             (taps[:], w_dw.rearrange("(k p) o -> p k o", p=P))):
                sp.dma_start(dst, src).then_inc(set_in, 16)
            for bk in range(NB * KT):
                with sp.Fori(0, NCHUNK // RING) as i:
                    for r in range(RING):
                        sp.wait_ge(chunk_used, i * RING + (bk * NCHUNK + r + 1))
                        sp.dma_start(acc[:, r].rearrange("p a b -> p (a b)"),
                                     xc[bk, :, bass.ds(i * (RING * CHUNK) + r * CHUNK, CHUNK)]
                                     ).then_inc(chunk_in[r], 16)

            def store(S, R):
                w, w0 = S - 2, R - 2
                if w0 < 0:
                    return
                for m in range(KT):
                    parts = y_parts(w, w0)
                    sp.wait_ge(res_in[m], (stores_before(w, w0) + len(parts)) * 16)
                    for b, top, r0, nr in parts:
                        sp.dma_start(orow[b * KT + m, :, bass.ds(top, nr)], y[:, m, r0:r0 + nr]
                                     ).then_inc(stored[m], 16)

            pipeline(sp, store)
            for m in range(KT):
                sp.wait_ge(stored[m], 16 * stores_before(NS + 1, NS + 1))

        @block.gpsimd
        def _(pool):
            nc.gpsimd.memset(t_buf[:], 0.0).then_inc(zeroed, 1)
            nc.gpsimd.memset(edge[:], 0.0).then_inc(zeroed, 1)
            nc.gpsimd.memset(zrows[:], 0.0).then_inc(zeroed, 1)

            def add_x(S, R):
                w, w0 = S - 2, R - 2
                if w0 < 0:
                    return
                for m in range(KT):
                    pool.wait_ge(y_ready, w * (KT * NG) + (m + 1) * (1 if w0 == NS else NG))
                    for b, top, r0, nr in y_parts(w, w0):
                        pool.dma_start(y[:, m, r0:r0 + nr], xr[b * KT + m, :, bass.ds(top, nr)],
                                       accum_op=ALU.add).then_inc(res_in[m], 16)

            pipeline(pool, add_x)

        @block.tensor
        def _(pe):
            pe.wait_ge(set_in, 144)
            nc.tensor.matmul(ps[:, 0, 0:CH], sel_s, filt_s, start=True, stop=True).then_inc(gp, 1)
            for n, row in ((1, 0), (2, 2)):
                pe.wait_ge(gs, 1 if n == 1 else 4)
                for k in range(KT):
                    for c in range(KT):
                        mm = nc.tensor.matmul(ps[:, n, k * NB:(k + 1) * NB], gmean_s[:, c, k * P:(k + 1) * P],
                                              gst[:, row, c * NB:(c + 1) * NB],
                                              start=(c == 0), stop=(c == KT - 1))
                mm.then_inc(gp, 1)
            pe.wait_ge(wi_ready, NB * KT)
            for b in range(NB):
                for k in range(KT):
                    for c in range(KT):
                        mm = nc.tensor.matmul(ps[:, 3, b * KT + k:b * KT + k + 1], wi[:, b, c, k * P:(k + 1) * P],
                                              gst[:, 9, c * NB + b:c * NB + b + 1],
                                              start=(c == 0), stop=(c == KT - 1))
            mm.then_inc(gp, 1)
            pe.wait_ge(beta_ready, 1)

            def stage_a(Sg, b, j, h):
                G = Sg * NG + j
                if h == 0:
                    pe.wait_ge(xp_ready, G * KT + KT)
                wait(pe, tf_ready, G * 2 + (h - 1))
                for q in range(2):
                    for k in range(KT):
                        mm = nc.tensor.matmul(ps[:, 2 * h + q, 0:CH], xp[:, j % 2, k, 2 * h + q],
                                              wi[:, b, k, :], start=(k == 0), stop=(k == KT - 1))
                mm.then_inc(a_done, 1)

            def stage_b(Sg, j, h):
                pe.wait_ge(ta_ready, (Sg * NG + j) * 2 + (h + 1))
                for q in range(2):
                    mm = nc.tensor.matmul(ps[:, 2 * h + q, 0:CH], dft_s[:], ta[:, h, q, :], start=True, stop=True)
                mm.then_inc(b_done, 1)

            def stage_d(S, R, p):
                G, G0 = S * NG + p, R * NG + p
                pe.wait_ge(tf_ready, G * 2 + 2)
                for k in range(KT):
                    if k == 0:
                        wait(pe, t_ready, G * KT)
                    elif G0 > 2 * NG:
                        pe.wait_ge(y_ready, G * KT - (2 * NG + 1) * KT + k)
                    bank = ps[:, 4 + (2 * p + k) % 4].rearrange("p (r c) -> p r c", c=GC)
                    for q in range(NPAIR):
                        mm = nc.tensor.matmul(bank[:, :, q * PC:(q + 1) * PC],
                                              tf[:, p % 2, q // 2, q % 2, k * P:(k + 1) * P], dftt_s[:],
                                              start=True, stop=True)
                    mm.then_inc(d_done, 1)

            def stage_w(S, R, p):
                w, w0 = S - 2, R - 2
                G = S * NG + p
                rows = win_rows(w0)
                cols = W if w0 == NS else GC
                if p == 0:
                    pe.wait_ge(g_ready, w * 2 + 2)
                for i in range(KT):
                    u = KT * p + i
                    m, n = (i, 0) if w0 == NS else (u // NG, u % NG)
                    if i == 0:
                        wait(pe, y_ready, G * KT - 2 * NG * KT)
                    elif R < NS:
                        pe.wait_ge(t_ready, G * KT + i)
                    o = ps[:, 4 + (2 * p + 3 + i) % 4, 0:rows * cols].rearrange("p (r c) -> p r c", c=cols)
                    nc.tensor.matmul(o, wo[:, 0, m * P:(m + 1) * P],
                                     acc[:, acc_of(1, w0), 0:rows, n * GC:n * GC + cols], start=True, stop=False)
                    nc.tensor.matmul(o, wo[P - LO:P, 1, m * P:(m + 1) * P],
                                     acc[P - LO:P, acc_of(2, w0), 0:rows, n * GC:n * GC + cols],
                                     start=False, stop=True).then_inc(w_done, 1)

            def step(S, R):
                for p in range(NG):
                    Sg, Rg, j = (S, R, p + 1) if p < NG - 1 else (S + 1, R + 1, 0)
                    if Rg < NS:
                        for h in range(2):
                            stage_a(Sg, Rg // STRIPS, j, h)
                        for h in range(2):
                            stage_b(Sg, j, h)
                    if R < NS:
                        stage_d(S, R, p)
                    elif p == 0 and R == NS:
                        pe.wait_ge(t_ready, NS * NG * KT)
                    if R >= 2 and (R < NS + 2 or p == 0):
                        stage_w(S, R, p)

            for h in range(2):
                stage_a(0, 0, 0, h)
            for h in range(2):
                stage_b(0, 0, h)
            pipeline(pe, step)

        @block.scalar
        def _(act):
            def load(Sg, Rg, h):
                if Rg >= NS:
                    return
                if Rg > 0:
                    act.wait_ge(xp_ready, Sg * (NG * KT) + (h - 1) * (NG * KT // 2))
                b = Rg // STRIPS
                for k in range(KT):
                    act.dma_start(xh[:, h, k], xr[b * KT + k, :, bass.ds((Sg - b * STRIPS) * EDGE, EDGE),
                                                  h * HC:(h + 1) * HC]).then_inc(x_in[h], 16)

            for h in range(2):
                load(0, 0, h)
            act.wait_ge(gs, 5)
            nc.scalar.activation(gst[:, 5], gst[:, 4], ACT.Sqrt).then_inc(ga, 1)
            act.wait_ge(zeroed, 3)
            act.wait_ge(beta_ready, 1)

            def pair_x(Sg, Rg, j):
                if Rg >= NS:
                    return
                if j % 2 == 0:
                    act.wait_ge(x_in[j // 2], Sg * (16 * KT) + 16 * KT)
                wait(act, a_done, (Sg * NG + j) * 2 - 2)
                for k in range(KT):
                    nc.scalar.activation(
                        xp[:, j % 2, k].rearrange("p q (r c) -> p q r c", c=PC),
                        xh[:, j // 2, k, :, (j % 2) * GC:(j % 2 + 1) * GC].rearrange("p r (q c) -> p q r c", c=PC),
                        ACT.Identity).then_inc(xp_ready, 1)

            def evacuate_a(Sg, j, h):
                G = Sg * NG + j
                act.wait_ge(a_done, G * 2 + (h + 1))
                wait(act, b_done, G * 2 + (h - 1))
                nc.scalar.activation(ta[:, h], ps[:, 2 * h:2 * h + 2, 0:CH], ACT.Identity).then_inc(ta_ready, 1)

            def evacuate_d(S, R, p):
                for k in range(KT):
                    act.wait_ge(d_done, (S * NG + p) * KT + (k + 1))
                    if p == 0 and R > 1:
                        act.wait_ge(tap[k], taps_before(k, S - 1, R - 1))
                        if k == 2:
                            act.wait_ge(g_ready, S * 2 - 3)
                    nc.scalar.activation(t_buf[:, R % 2, k, 2:2 + EDGE, 1 + p * GC:1 + (p + 1) * GC],
                                         ps[:, 4 + (2 * p + k) % 4].rearrange("p (r c) -> p r c", c=GC),
                                         ACT.Identity, bias=beta[:, R // STRIPS, k:k + 1]).then_inc(t_ready, 1)

            def evacuate_w(S, R, p):
                w, w0 = S - 2, R - 2
                rows = win_rows(w0)
                cols = W if w0 == NS else GC
                for i in range(KT):
                    u = KT * p + i
                    m, n = (i, 0) if w0 == NS else (u // NG, u % NG)
                    act.wait_ge(w_done, (S * NG + p) * KT - 2 * NG * KT + (i + 1))
                    if n == 0 and w0 > 0:
                        act.wait_ge(stored[m], stores_before(w, w0) * 16)
                    nc.scalar.activation(y[:, m, 0:rows, n * GC:n * GC + cols],
                                         ps[:, 4 + (2 * p + 3 + i) % 4, 0:rows * cols
                                            ].rearrange("p (r c) -> p r c", c=cols),
                                         ACT.Identity).then_inc(y_ready, 1)

            def halo(S, R, k):
                last_rows = t_buf[:, (R - 1) % 2, k, EDGE:EDGE + 2]
                act.wait_ge(t_ready, S * (NG * KT))
                if R > 1:
                    act.wait_ge(tap[k], taps_before(k, S - 1, R - 1))
                if R % STRIPS == 0:
                    nc.scalar.activation(edge[:, k], last_rows, ACT.Identity).then_inc(edge_ready, 1)
                    last_rows = zrows[:]
                if R < NS:
                    nc.scalar.activation(t_buf[:, R % 2, k, 0:2], last_rows, ACT.Identity).then_inc(halo_ready, 1)

            def center(S, R, k):
                w, w0 = S - 1, R - 1
                act.wait_ge(t_ready, min(R, NS) * (NG * KT) if R >= NS else S * (NG * KT))
                wait(act, halo_ready, (min(w0, NS - 1) if w0 >= NS - 1 else w) * KT)
                if begins(w0) or w0 == NS:
                    wait(act, edge_ready, w0 // STRIPS * KT)
                if w0 >= 2:
                    act.wait_ge(w_done, (w - 1) * (KT * NG))
                ops = dw_ops(w0, k)[0]
                for n, (a, src, wt) in enumerate(ops):
                    nc.scalar.activation(a, src, ACT.Copy, scale=wt).then_inc(center_ready[k], 1)

            def gelu(S, R, k):
                w, w0 = S - 1, R - 1
                r = win_rows(w0)
                act.wait_ge(tap[k], taps_before(k, w + 1, w0 + 1))
                if k == 0:
                    nc.scalar.activation(acc[:, ACC0, 0:r], acc[:, ACC0, 0:r], ACT.Gelu).then_inc(gelu_ready, 1)
                else:
                    nc.scalar.activation(gelu2(w0, r), acc[0:LO, acc_of(2, w0), 0:r],
                                         ACT.Gelu).then_inc(gelu_ready, 1)

            def step(S, R):
                for p in range(NG):
                    Sg, Rg, j = (S, R, p + 1) if p < NG - 1 else (S + 1, R + 1, 0)
                    dw = 1 <= R <= NS + 1
                    if p % 2 == 0:
                        load(S + 1, R + 1, p // 2)
                    if p < NG - 2:
                        pair_x(S, R, p + 2)
                    else:
                        pair_x(S + 1, R + 1, p + 2 - NG)
                    if dw and p == 0:
                        center(S, R, 2)
                    if dw and p == 3:
                        gelu(S, R, 0)
                    if Rg < NS:
                        evacuate_a(Sg, j, 0)
                    if dw and p == 0:
                        center(S, R, 1)
                    if dw and p == 3:
                        gelu(S, R, 2)
                    if Rg < NS:
                        evacuate_a(Sg, j, 1)
                    if p > 0 and 1 <= R <= NS:
                        halo(S, R, p - 1)
                    if R < NS:
                        evacuate_d(S, R, p)
                    if R >= 2 and (R < NS + 2 or p == 0):
                        evacuate_w(S, R, p)

            pair_x(0, 0, 0)
            pair_x(0, 0, 1)
            for h in range(2):
                evacuate_a(0, 0, h)
            pipeline(act, step)

        @block.vector
        def _(dve):
            for bk in range(NB * KT):
                wait(dve, stat_ready, bk)
                if bk == 0:
                    nc.vector.memset(gst[:], 0.0).then_inc(chunk_used, RING)
                with dve.Fori(0, NCHUNK // RING) as i:
                    for r in range(RING):
                        dve.wait_ge(chunk_in[r], i * 16 + (bk * (NCHUNK // RING) + 1) * 16)
                        for n in range(CHUNK // BN):
                            at = i * (RING * CHUNK // BN * 6) + (r * (CHUNK // BN) + n) * 6
                            ins = nc.vector.bn_stats(bnst[:, bass.ds(at, 6)],
                                                     acc[:, r].rearrange("p a b -> p (a b)")[:, n * BN:(n + 1) * BN])
                        ins.then_inc(chunk_used, 1)
                dve.wait_ge(chunk_used, RING + (bk + 1) * NCHUNK)
                nc.vector.bn_aggr(mv[:, bk], bnst).then_inc(stat_ready, 1)
            dve.wait_ge(stat_ready, NB * KT)

            done = [0]

            def link(ins):
                done[0] += 1
                ins.then_inc(gs, 1)
                dve.wait_ge(gs, done[0])

            def stat(n):
                return mv[:].rearrange("p (b k) n -> p k b n", b=NB)[:, :, :, n]

            def row(n):
                return gst[:, n].rearrange("p (k b) -> p k b", b=NB)

            dve.wait_ge(gp, 1)
            for q in range(2):
                nc.vector.tensor_copy(fil[:, q], ps[:, 0, 0:CH]).then_inc(stat_ready, 1)
            link(nc.vector.tensor_copy(row(0), stat(0)))
            dve.wait_ge(gp, 2)
            gm = ps[:, 1, 0:NB * KT]
            link(nc.vector.tensor_tensor(gst[:, 1], gst[:, 0], gm, ALU.subtract))
            link(nc.vector.tensor_tensor(gst[:, 3], gst[:, 1], gst[:, 1], ALU.mult))
            link(nc.vector.tensor_tensor(row(2), row(3), stat(1), ALU.add))
            dve.wait_ge(gp, 3)
            link(nc.vector.tensor_scalar(gst[:, 4], ps[:, 2, 0:NB * KT], EPS, None, ALU.add))
            dve.wait_ge(ga, 1)
            link(nc.vector.reciprocal(gst[:, 6], gst[:, 5]))
            link(nc.vector.tensor_tensor(gst[:, 7], gst[:, 6], gst[:, 6], ALU.mult))
            link(nc.vector.tensor_tensor(gst[:, 8], gst[:, 7], gst[:, 4], ALU.mult))
            link(nc.vector.tensor_scalar(gst[:, 7], gst[:, 8], -0.5, 1.5, ALU.mult, ALU.add))
            link(nc.vector.tensor_tensor(gst[:, 8], gst[:, 6], gst[:, 7], ALU.mult))
            link(nc.vector.tensor_scalar(gst[:, 9], gm, -1.0, None, ALU.mult))
            for b in range(NB):
                for k in range(KT):
                    nc.vector.tensor_scalar(wi[:, b, k], wraw[:, k], gst[:, 8, k * NB + b:k * NB + b + 1], None,
                                            ALU.mult).then_inc(wi_ready, 1)
            dve.wait_ge(gp, 4)
            for b in range(NB):
                ins = nc.vector.tensor_tensor(beta[:, b], ps[:, 3, b * KT:(b + 1) * KT], taps[:, :, 9], ALU.mult)
            ins.then_inc(beta_ready, 1)
            dve.wait_ge(zeroed, 3)

            def stage_c(Sg, j, h):
                G = Sg * NG + j
                dve.wait_ge(b_done, G * 2 + (h + 1))
                wait(dve, d_done, G * KT - KT)
                nc.vector.tensor_tensor(tf[:, j % 2, h], ps[:, 2 * h:2 * h + 2, 0:CH], fil[:],
                                        ALU.mult).then_inc(tf_ready, 1)

            def window(S, R):
                w, w0 = S - 1, R - 1
                r = win_rows(w0)

                def first(k, op):
                    dst, src, wt = op
                    if w0 < NS:
                        dve.wait_ge(t_ready, S * (NG * KT))
                        wait(dve, halo_ready, w * KT)
                    if begins(w0) or w0 == NS:
                        wait(dve, edge_ready, w0 // STRIPS * KT)
                    wait(dve, g_ready, w * 2)
                    nc.vector.tensor_scalar(dst, src, wt, None, ALU.mult).then_inc(tap[k], 1)

                def other(k, n, op):
                    dst, src, wt = op
                    if n == 0:
                        if w0 == NS or begins(w0):
                            dve.wait_ge(center_ready[k], w + firsts(w0) + (1 if w0 == NS else 2))
                        else:
                            dve.wait_ge(center_ready[k], w + firsts(w0) + 1)
                    wait(dve, tap[k], taps_before(k, w, w0) + n)
                    nc.vector.scalar_tensor_tensor(dst, src, wt, dst, ALU.mult, ALU.add).then_inc(tap[k], 1)

                def product(k):
                    dve.wait_ge(gelu_ready, w * 2 + (1 if k == 0 else 2))
                    if k == 0:
                        dve.wait_ge(tap[1], taps_before(1, w + 1, w0 + 1))
                        a = acc[:, acc_of(1, w0), 0:r]
                        nc.vector.tensor_tensor(a, a, acc[:, ACC0, 0:r], ALU.mult).then_inc(g_ready, 1)
                    else:
                        a = acc[P - LO:P, acc_of(2, w0), 0:r]
                        nc.vector.tensor_tensor(a, a, gelu2(w0, r), ALU.mult).then_inc(g_ready, 1)

                todo = {}
                for k in range(KT):
                    centers, others = dw_ops(w0, k)
                    todo[k] = []
                    if k == 0:
                        todo[k] += [lambda k=k, o=o: first(k, o) for o in centers]
                    n0 = len(todo[k])
                    todo[k] += [lambda k=k, n=n, o=o, n0=n0: other(k, n + n0, o) for n, o in enumerate(others)]
                ops = []
                for n in range(max(len(todo[0]), len(todo[2]))):
                    for k in (0, 2):
                        ops += todo[k][n:n + 1]
                ops += todo[1][:5] + [lambda: product(2)] + todo[1][5:] + [lambda: product(0)]
                return ops

            def step(S, R):
                ops = window(S, R) if 1 <= R <= NS + 1 else []
                for p in range(NG):
                    mine = ops[len(ops) * p // NG:len(ops) * (p + 1) // NG]
                    Sg, Rg, j = (S, R, p + 1) if p < NG - 1 else (S + 1, R + 1, 0)
                    ahead = len(mine) * 4 // 7
                    for op in mine[:ahead]:
                        op()
                    if Rg < NS:
                        stage_c(Sg, j, 0)
                    for op in mine[ahead:ahead + 1]:
                        op()
                    if Rg < NS:
                        stage_c(Sg, j, 1)
                    for op in mine[ahead + 1:]:
                        op()

            for h in range(2):
                stage_c(0, 0, h)
            pipeline(dve, step)


def _constants(np):
    rows = np.arange(EDGE)
    basis, entries = [], []
    for k1 in range(EDGE):
        for k2 in range(EDGE // 2 + 1):
            angle = 2 * np.pi * (k1 * rows[:, None] + k2 * rows[None, :]) / EDGE
            k1n = (-k1) % EDGE
            own = k2 in (0, EDGE // 2)
            weight = np.zeros((EDGE, EDGE // 2 + 1))
            if own and k1 == k1n:
                weight[k1, k2] = 1.0
                basis.append(np.cos(angle) / EDGE)
                entries.append(weight)
            elif not own or k1 < k1n:
                weight[k1, k2] += 0.5 if own else 1.0
                if own:
                    weight[k1n, k2] += 0.5
                for f in (np.cos(angle), np.sin(angle)):
                    basis.append(f * np.sqrt(2.0) / EDGE)
                    entries.append(weight)
    basis = np.stack(basis)
    n = len(basis)
    dft = np.zeros((EDGE, 2, EDGE, 2, n))
    for patch in range(2):
        dft[:, patch, :, patch, :] = basis.transpose(1, 2, 0)
    dft = dft.reshape(P, P).astype(np.float32)
    entries = np.stack(entries).reshape(n, -1)
    select = np.concatenate([entries, entries]).T.astype(np.float32)
    group = np.arange(CH) // CPG
    group_mean = ((group[:, None] == group[None, :]) / CPG).astype(np.float32)
    return {"dft": dft, "dft_t": dft.T, "select": select, "group_mean": group_mean}


def kernel(x, L0_conv_fft_filter, L0_conv_w_in, L0_conv_w_dw, L0_conv_w_out):
    import numpy as np
    import concourse.bacc as bacc
    from concourse.bass_utils import run_bass_kernel_spmd as run

    order = np.concatenate([np.arange(P), HID2 + np.arange(P), np.arange(P, HID2), HID2 + np.arange(P, HID2)])
    w_in, w_dw, w_out = np.asarray(L0_conv_w_in), np.asarray(L0_conv_w_dw), np.asarray(L0_conv_w_out)
    fft = np.asarray(L0_conv_fft_filter)
    arrays = {
        "x": np.asarray(x),
        "w_in": w_in[order].T,
        "w_out": w_out.T,
        "w_dw": np.concatenate([w_dw[order].reshape(CH, 9), fft[order][:, 0, 0:1]], axis=1),
        "filt": fft[order].reshape(CH, -1).T,
        **_constants(np),
    }
    arrays = {f"in_{k}": np.ascontiguousarray(v) for k, v in arrays.items()}
    nc = bacc.Bacc("TRN2", target_bir_lowering=False, num_devices=1)
    args = [nc.dram_tensor(n, a.shape, mybir.dt.from_np(a.dtype), kind="ExternalInput").ap()
            for n, a in arrays.items()]
    out = nc.dram_tensor("out", (NB, CH, H, W), F32, kind="ExternalOutput").ap()
    conv_kernel(nc, *args, out)
    r = run(nc, [arrays], core_ids=[0])
    return r.results[0]["out"]
```

```python
from contextlib import ExitStack

import concourse.bass as bass
from concourse import mybir

F32 = mybir.dt.float32
ALU = mybir.AluOpType
ACT = mybir.ActivationFunctionType

P = 128
EDGE = 8
NB, CH, H, W = 2, 384, 256, 256
KT = CH // P
GROUPS = 32
CPG = CH // GROUPS
EPS = 1e-5
STRIPS = H // EDGE
NS = NB * STRIPS
GC = 64
NG = W // GC
PC = 16
NPAIR = GC // PC
HC = W // 2
TW = W + 2
WIN = EDGE * W
BN = 512
CHUNK = WIN
NCHUNK = H * W // CHUNK
RING = 4
FIRST = 3
PER_TILE = NCHUNK // NG
NSUM = KT * NCHUNK
HID2 = CH // 2
LO = HID2 - P

GSTEPS = 11

ACC0, ACC1, ACC2, NACC = 0, (1, 2), (3, 4), 5


def acc_of(tile, w):
    return ACC0 if tile == 0 else (ACC1, ACC2)[tile - 1][w % 2]


def begins(w):
    return w < NS and w % STRIPS == 0


def firsts(w):
    return (w + STRIPS - 1) // STRIPS if w < NS else NB


def n_taps(tile, w):
    per = 8 if tile else 9
    edge_taps = 5 if tile else 6
    return edge_taps if w == NS else per + (edge_taps if begins(w) else 0)


def taps_before(tile, w, w0):
    if w0 == NS + 1:
        return taps_before(tile, NS, NS) + n_taps(tile, NS)
    return w * n_taps(tile, 1) + firsts(w0) * (n_taps(tile, 0) - n_taps(tile, 1))


def stores_before(w, w0):
    return w + sum(1 for b in range(1, NB) if w0 > b * STRIPS)


def conv_kernel(nc, x, w_in, w_out, w_dw, filt, dft, dft_t, select, group_mean, out):
    xc = x.rearrange("b (k p) h w -> (b k) p (h w)", p=P)
    orow = out.rearrange("b (k p) h w -> (b k) p h w", p=P)
    xr = x.rearrange("b (k p) h w -> (b k) p h w", p=P)

    with ExitStack() as ctx:
        def sb(name, shape, dt=F32):
            return ctx.enter_context(nc.sbuf_tensor(name, shape, dt))

        def sem(name):
            return ctx.enter_context(nc.semaphore(name))

        t_buf = sb("t_buf", [P, 2, KT, EDGE + 2, TW])
        edge = sb("edge", [P, KT, 2, TW])
        acc = sb("acc", [P, NACC, EDGE, W])
        y = sb("y", [P, 2, EDGE, W])
        xh = sb("xh", [P, 2, KT, EDGE, HC])
        xp = sb("xp", [P, KT, NPAIR, EDGE * PC])
        xs = sb("xs", [P, CHUNK])
        ta = sb("ta", [P, 2, 2, CH])
        tf = sb("tf", [P, 2, 2, 2, CH])
        wi = sb("wi", [P, NB, KT, CH])
        wo = sb("wo", [P, 2, CH])
        fil = sb("fil", [P, 2, CH])
        dft_s = sb("dft_s", [P, P])
        dftt_s = sb("dftt_s", [P, P])
        taps = sb("taps", [P, KT, 10])
        beta = sb("beta", [P, NB, KT])
        mv = sb("mv", [P, NB, KT, 2])
        gst = sb("gst", [P, NB, 10, KT])
        sample = sb("sample", [P, KT, 2])
        shift = sb("shift", [P, KT])
        sums = sb("sums", [P, 2, NSUM])
        total = sb("total", [P, 2, KT])
        gmean_s = xs[:, 0:KT * CH].rearrange("p (k c) -> p k c", k=KT)
        y0 = y[:, 0].rearrange("p a b -> p (a b)")
        y1 = y[:, 1].rearrange("p a b -> p (a b)")
        bnst = y0[:, 0:NCHUNK * (CHUNK // BN) * 6]
        sel_s = y1[0:40, 0:P]
        filt_s = y1[0:40, P:P + CH]
        bnsamp = y1[:, P + CH:P + CH + 6 * KT].rearrange("p (k n) -> p k n", k=KT)
        samp_s = acc[:, NACC - 1].rearrange("p a b -> p (a b)")[:, 0:KT * BN].rearrange("p (k n) -> p k n", k=KT)

        ps = ctx.enter_context(nc.psum_tensor("ps", [P, 8, 512], F32))

        set_in = sem("set_in")
        chunk_in = [sem(f"chunk_in{r}") for r in range(RING)]
        chunk_used = sem("chunk_used")
        xs_in = sem("xs_in")
        xs_used = sem("xs_used")
        reduced = sem("reduced")
        stat_ready = sem("stat_ready")
        gs = sem("gs")
        filter_made = sem("filter_made")
        fil_ready = sem("fil_ready")
        gp = sem("gp")
        ga = sem("ga")
        wi_ready = sem("wi_ready")
        beta_ready = sem("beta_ready")
        zeroed = sem("zeroed")
        edge_ready = sem("edge_ready")
        x_in = [sem("x_in0"), sem("x_in1")]
        xp_ready = sem("xp_ready")
        a_done = sem("a_done")
        ta_ready = sem("ta_ready")
        b_done = sem("b_done")
        tf_ready = sem("tf_ready")
        d_done = sem("d_done")
        t_ready = sem("t_ready")
        halo_ready = sem("halo_ready")
        center_ready = [sem(f"center_ready{k}") for k in range(KT)]
        tap = [sem(f"tap{k}") for k in range(KT)]
        gelu_ready = sem("gelu_ready")
        g_ready = sem("g_ready")
        w_done = sem("w_done")
        y_ready = sem("y_ready")
        res_in = [sem(f"res_in{m}") for m in range(KT)]
        stored = [sem(f"stored{m}") for m in range(KT)]

        def wait(eng, s, value):
            if not isinstance(value, int) or value > 0:
                eng.wait_ge(s, value)

        def pipeline(eng, step):
            def loop(first, n):
                if n:
                    with eng.Fori(0, n // 2) as i:
                        for u in (first, first + 1):
                            step(i * 2 + u, u)

            for b in range(NB):
                s0 = b * STRIPS
                for S in range(s0, s0 + FIRST):
                    step(S, S)
                if b == 0:
                    for k in range(KT):
                        loop(FIRST + k * PER_TILE, PER_TILE)
                    loop(FIRST + KT * PER_TILE, STRIPS - 1 - FIRST - KT * PER_TILE)
                else:
                    loop(s0 + FIRST, STRIPS - 1 - FIRST)
                step(s0 + STRIPS - 1, s0 + STRIPS - 1)
            for S in range(NS, NS + 3):
                step(S, S)

        def dw_rows(w0, k):
            par = w0 % 2
            whole = (0, EDGE, lambda di, r: t_buf[:, par, k, 1 + di + r:1 + di + r + EDGE], (-1, 0, 1))
            if w0 == NS:
                return [(0, 1, lambda di, r: edge[:, k, 1 + di:2 + di], (-1, 0))]
            if begins(w0):
                return [(1, EDGE - 1, lambda di, r: t_buf[:, par, k, 2 + di:1 + di + EDGE], (-1, 0, 1)),
                        (0, 1, lambda di, r: edge[:, k, 1 + di:2 + di], (-1, 0))]
            return [whole]

        def dw_ops(w0, k):
            ops = []
            for r0, nr, source, dis in dw_rows(w0, k):
                for di in dis:
                    for dj in (-1, 0, 1):
                        ops.append((acc[:, acc_of(k, w0), r0:r0 + nr], source(di, 0)[:, :, 1 + dj:1 + dj + W],
                                    taps[:, k, (di + 1) * 3 + dj + 1:(di + 1) * 3 + dj + 2], di == 0 and dj == 0))
            return [o[:3] for o in ops if o[3]], [o[:3] for o in ops if not o[3]]

        def gelu2(w0, rows):
            return t_buf[P - LO:P, w0 % 2, 2, 0:rows, 1:1 + W]

        def y_parts(w, w0):
            b = min(w0 // STRIPS, NB - 1)
            if w0 < NS and not begins(w0):
                return [(b, (w - b * STRIPS) * EDGE - 1, 0, EDGE)]
            parts = [(b, 0, 1, EDGE - 1)] if w0 < NS else []
            return parts + [((w0 - 1) // STRIPS, H - 1, 0, 1)] * (w0 > 0)

        def win_rows(w0):
            return 1 if w0 == NS else EDGE

        block = ctx.enter_context(nc.Block())

        @block.sync
        def _(sp):
            for dst, src in ((wi[:, NB - 1], w_in.rearrange("(k p) o -> p k o", p=P)),
                             (gmean_s, group_mean.rearrange("(k p) o -> p k o", p=P)),
                             (wo[:, 0], w_out[0:P]),
                             (wo[P - LO:P, 1], w_out[P:HID2]),
                             (dft_s[:], dft), (dftt_s[:], dft_t), (sel_s, select), (filt_s, filt),
                             (taps[:], w_dw.rearrange("(k p) o -> p k o", p=P)),
                             (samp_s, xc[KT:2 * KT, :, 0:BN].rearrange("k p n -> p k n"))):
                sp.dma_start(dst, src).then_inc(set_in, 16)
            for k in range(KT):
                with sp.Fori(0, NCHUNK // RING) as i:
                    for r in range(RING):
                        sp.wait_ge(chunk_used, i * RING + (k * NCHUNK + r + 1))
                        sp.dma_start(acc[:, r].rearrange("p a b -> p (a b)"),
                                     xc[k, :, bass.ds(i * (RING * CHUNK) + r * CHUNK, CHUNK)]
                                     ).then_inc(chunk_in[r], 16)

            def store(S, R):
                w, w0 = S - 2, R - 2
                if w0 < 0:
                    return
                for m in range(KT):
                    parts = y_parts(w, w0)
                    sp.wait_ge(res_in[m], (stores_before(w, w0) + len(parts)) * 16)
                    for b, top, r0, nr in parts:
                        sp.dma_start(orow[b * KT + m, :, bass.ds(top, nr)], y[:, (w0 + m) % 2, r0:r0 + nr]
                                     ).then_inc(stored[m], 16)

            pipeline(sp, store)
            for m in range(KT):
                sp.wait_ge(stored[m], 16 * stores_before(NS + 1, NS + 1))

        @block.gpsimd
        def _(pool):
            nc.gpsimd.memset(t_buf[:], 0.0).then_inc(zeroed, 1)
            nc.gpsimd.memset(edge[:], 0.0).then_inc(zeroed, 1)

            def add_x(S, R):
                w, w0 = S - 2, R - 2
                if w0 < 0:
                    return
                for m in range(KT):
                    pool.wait_ge(y_ready, w * (KT * NG) + (m + 1) * (1 if w0 == NS else NG))
                    for b, top, r0, nr in y_parts(w, w0):
                        pool.dma_start(y[:, (w0 + m) % 2, r0:r0 + nr], xr[b * KT + m, :, bass.ds(top, nr)],
                                       accum_op=ALU.add).then_inc(res_in[m], 16)

            pipeline(pool, add_x)

        @block.tensor
        def _(pe):
            pe.wait_ge(set_in, 160)
            nc.tensor.matmul(ps[:, 7, 0:CH], sel_s, filt_s, start=True, stop=True).then_inc(filter_made, 1)

            def small(b, n, bank):
                if n < 2:
                    pe.wait_ge(gs, b * GSTEPS + (1, 5)[n])
                else:
                    pe.wait_ge(wi_ready, (b + 1) * KT)
                for k in range(KT):
                    for c in range(KT):
                        lhs = (gmean_s if n < 2 else wi[:, b])[:, c, k * P:(k + 1) * P]
                        mm = nc.tensor.matmul(ps[:, bank, k:k + 1], lhs, gst[:, b, (0, 3, 9)[n], c:c + 1],
                                              start=(c == 0), stop=(c == KT - 1))
                mm.then_inc(gp, 1)

            for n in range(3):
                small(0, n, 4 + n)

            def stage_a(Sg, b, j, h):
                G = Sg * NG + j
                if h == 0:
                    pe.wait_ge(xp_ready, G * KT + KT)
                wait(pe, tf_ready, G * 2 + (h - 1))
                for q in range(2):
                    for k in range(KT):
                        mm = nc.tensor.matmul(ps[:, 2 * h + q, 0:CH], xp[:, k, 2 * h + q],
                                              wi[:, b, k, :], start=(k == 0), stop=(k == KT - 1))
                mm.then_inc(a_done, 1)

            def stage_b(Sg, j, h):
                pe.wait_ge(ta_ready, (Sg * NG + j) * 2 + (h + 1))
                for q in range(2):
                    mm = nc.tensor.matmul(ps[:, 2 * h + q, 0:CH], dft_s[:], ta[:, h, q, :], start=True, stop=True)
                mm.then_inc(b_done, 1)

            def stage_d(S, R, p):
                G, G0 = S * NG + p, R * NG + p
                pe.wait_ge(tf_ready, G * 2 + 2)
                if G0 == 0:
                    pe.wait_ge(beta_ready, 1)
                    pe.wait_ge(fil_ready, 2)
                if R == STRIPS - 1 and p > 0:
                    pe.wait_ge((gs, gs, beta_ready)[p - 1], (GSTEPS + 2, GSTEPS + 6, 2)[p - 1])
                for k in range(KT):
                    if k == 0:
                        wait(pe, t_ready, G * KT)
                    elif G0 > 2 * NG:
                        pe.wait_ge(y_ready, G * KT - (2 * NG + 1) * KT + k)
                    bank = ps[:, 4 + (2 * p + k) % 4].rearrange("p (r c) -> p r c", c=GC)
                    for q in range(NPAIR):
                        mm = nc.tensor.matmul(bank[:, :, q * PC:(q + 1) * PC],
                                              tf[:, p % 2, q // 2, q % 2, k * P:(k + 1) * P], dftt_s[:],
                                              start=True, stop=True)
                    mm.then_inc(d_done, 1)

            def stage_w(S, R, p):
                w, w0 = S - 2, R - 2
                G = S * NG + p
                rows = win_rows(w0)
                cols = W if w0 == NS else GC
                if p == 0:
                    pe.wait_ge(g_ready, w * 2 + 2)
                for i in range(KT):
                    u = KT * p + i
                    m, n = (i, 0) if w0 == NS else (u // NG, u % NG)
                    if i == 0:
                        wait(pe, y_ready, G * KT - 2 * NG * KT)
                    elif R < NS:
                        pe.wait_ge(t_ready, G * KT + i)
                    o = ps[:, 4 + (2 * p + 3 + i) % 4, 0:rows * cols].rearrange("p (r c) -> p r c", c=cols)
                    nc.tensor.matmul(o, wo[:, 0, m * P:(m + 1) * P],
                                     acc[:, acc_of(1, w0), 0:rows, n * GC:n * GC + cols], start=True, stop=False)
                    nc.tensor.matmul(o, wo[P - LO:P, 1, m * P:(m + 1) * P],
                                     acc[P - LO:P, acc_of(2, w0), 0:rows, n * GC:n * GC + cols],
                                     start=False, stop=True).then_inc(w_done, 1)

            def step(S, R):
                for p in range(NG):
                    Sg, Rg, j = (S, R, p + 1) if p < NG - 1 else (S + 1, R + 1, 0)
                    if R == STRIPS - 1 and p > 0:
                        if p == 1:
                            pe.wait_ge(xs_in, 16 * (NSUM + 1))
                        pe.wait_ge(t_ready, (S * NG + p) * KT)
                        small(1, p - 1, 4 + (2 * p) % 4)
                    if Rg < NS:
                        for h in range(2):
                            stage_a(Sg, Rg // STRIPS, j, h)
                        for h in range(2):
                            stage_b(Sg, j, h)
                    if R < NS:
                        stage_d(S, R, p)
                    elif p == 0 and R == NS:
                        pe.wait_ge(t_ready, NS * NG * KT)
                    if R >= 2 and (R < NS + 2 or p == 0):
                        stage_w(S, R, p)

            for h in range(2):
                stage_a(0, 0, 0, h)
            for h in range(2):
                stage_b(0, 0, h)
            pipeline(pe, step)

        @block.scalar
        def _(act):
            def load(Sg, Rg, h):
                if Rg >= NS:
                    return
                if Rg > 0:
                    act.wait_ge(xp_ready, Sg * (NG * KT) + (h - 1) * (NG * KT // 2))
                b = Rg // STRIPS
                for k in range(KT):
                    act.dma_start(xh[:, h, k], xr[b * KT + k, :, bass.ds((Sg - b * STRIPS) * EDGE, EDGE),
                                                  h * HC:(h + 1) * HC]).then_inc(x_in[h], 16)

            for h in range(2):
                load(0, 0, h)
            def root(b):
                act.wait_ge(gs, b * GSTEPS + 6)
                nc.scalar.activation(gst[:, b, 5], gst[:, b, 4], ACT.Sqrt).then_inc(ga, 1)

            root(0)
            act.wait_ge(zeroed, 2)
            act.wait_ge(beta_ready, 1)

            def load_chunk(S, R, p):
                n, k = (S - FIRST) * NG + p, (R - FIRST) // PER_TILE
                act.wait_ge(xs_used, n * 2 + 2)
                act.dma_start(xs[:], xc[KT + k, :, bass.ds(n * CHUNK - k * (NCHUNK * CHUNK), CHUNK)]
                              ).then_inc(xs_in, 16)

            def sum_chunk(S, R, p):
                n, k = (S - FIRST) * NG + p, (R - FIRST) // PER_TILE
                act.wait_ge(xs_in, n * 16 + 16)
                nc.scalar.activation(xs[:], xs[:], ACT.Identity, bias=shift[:, k:k + 1],
                                     accum_out=sums[:, 0, bass.ds(n, 1)]).then_inc(xs_used, 1)
                act.wait_ge(xs_used, n * 2 + 3)
                nc.scalar.activation(xs[:], xs[:], ACT.Square,
                                     accum_out=sums[:, 1, bass.ds(n, 1)]).then_inc(xs_used, 1)

            def pair_x(Sg, Rg, j):
                if Rg >= NS:
                    return
                if j % 2 == 0:
                    act.wait_ge(x_in[j // 2], Sg * (16 * KT) + 16 * KT)
                wait(act, a_done, (Sg * NG + j) * 2)
                for k in range(KT):
                    nc.scalar.activation(
                        xp[:, k].rearrange("p q (r c) -> p q r c", c=PC),
                        xh[:, j // 2, k, :, (j % 2) * GC:(j % 2 + 1) * GC].rearrange("p r (q c) -> p q r c", c=PC),
                        ACT.Identity).then_inc(xp_ready, 1)

            def evacuate_a(Sg, j, h):
                G = Sg * NG + j
                act.wait_ge(a_done, G * 2 + (h + 1))
                wait(act, b_done, G * 2 + (h - 1))
                nc.scalar.activation(ta[:, h], ps[:, 2 * h:2 * h + 2, 0:CH], ACT.Identity).then_inc(ta_ready, 1)

            def evacuate_d(S, R, p):
                for k in range(KT):
                    act.wait_ge(d_done, (S * NG + p) * KT + (k + 1))
                    if p == 0 and R > 1:
                        act.wait_ge(tap[k], taps_before(k, S - 1, R - 1))
                        if k == 2:
                            act.wait_ge(g_ready, S * 2 - 3)
                    nc.scalar.activation(t_buf[:, R % 2, k, 2:2 + EDGE, 1 + p * GC:1 + (p + 1) * GC],
                                         ps[:, 4 + (2 * p + k) % 4].rearrange("p (r c) -> p r c", c=GC),
                                         ACT.Identity, bias=beta[:, R // STRIPS, k:k + 1]).then_inc(t_ready, 1)

            def evacuate_w(S, R, p):
                w, w0 = S - 2, R - 2
                rows = win_rows(w0)
                cols = W if w0 == NS else GC
                for i in range(KT):
                    u = KT * p + i
                    m, n = (i, 0) if w0 == NS else (u // NG, u % NG)
                    act.wait_ge(w_done, (S * NG + p) * KT - 2 * NG * KT + (i + 1))
                    if n == 0 and m == 2:
                        act.wait_ge(stored[0], (stores_before(w, w0) + len(y_parts(w, w0))) * 16)
                    elif n == 0 and w0 > 0:
                        act.wait_ge(stored[m + 1], stores_before(w, w0) * 16)
                    nc.scalar.activation(y[:, (w0 + m) % 2, 0:rows, n * GC:n * GC + cols],
                                         ps[:, 4 + (2 * p + 3 + i) % 4, 0:rows * cols
                                            ].rearrange("p (r c) -> p r c", c=cols),
                                         ACT.Identity).then_inc(y_ready, 1)

            def halo(S, R, k):
                last_rows = t_buf[:, (R - 1) % 2, k, EDGE:EDGE + 2]
                act.wait_ge(t_ready, S * (NG * KT))
                if R > 1:
                    act.wait_ge(tap[k], taps_before(k, S - 1, R - 1))
                if R % STRIPS == 0:
                    nc.scalar.activation(edge[:, k], last_rows, ACT.Identity).then_inc(edge_ready, 1)
                    last_rows = t_buf[:, (R - 1) % 2, k, EDGE:EDGE + 2, 0:1].to_broadcast([P, 2, TW])
                if R < NS:
                    nc.scalar.activation(t_buf[:, R % 2, k, 0:2], last_rows, ACT.Identity).then_inc(halo_ready, 1)

            def center(S, R, k):
                w, w0 = S - 1, R - 1
                act.wait_ge(t_ready, min(R, NS) * (NG * KT) if R >= NS else S * (NG * KT))
                wait(act, halo_ready, (min(w0, NS - 1) if w0 >= NS - 1 else w) * KT)
                if begins(w0) or w0 == NS:
                    wait(act, edge_ready, w0 // STRIPS * KT)
                if w0 >= 2:
                    act.wait_ge(w_done, (w - 1) * (KT * NG))
                ops = dw_ops(w0, k)[0]
                for n, (a, src, wt) in enumerate(ops):
                    nc.scalar.activation(a, src, ACT.Copy, scale=wt).then_inc(center_ready[k], 1)

            def gelu(S, R, k):
                w, w0 = S - 1, R - 1
                r = win_rows(w0)
                act.wait_ge(tap[k], taps_before(k, w + 1, w0 + 1))
                if k == 0:
                    nc.scalar.activation(acc[:, ACC0, 0:r], acc[:, ACC0, 0:r], ACT.Gelu).then_inc(gelu_ready, 1)
                else:
                    nc.scalar.activation(gelu2(w0, r), acc[0:LO, acc_of(2, w0), 0:r],
                                         ACT.Gelu).then_inc(gelu_ready, 1)

            def step(S, R):
                for p in range(NG):
                    Sg, Rg, j = (S, R, p + 1) if p < NG - 1 else (S + 1, R + 1, 0)
                    dw = 1 <= R <= NS + 1
                    if p % 2 == 0:
                        load(S + 1, R + 1, p // 2)
                    stats = FIRST <= R < FIRST + KT * PER_TILE
                    if stats:
                        load_chunk(S, R, p)
                    if R == STRIPS - 1 and p == 0:
                        act.wait_ge(xs_used, 2 + 2 * NSUM)
                        act.dma_start(gmean_s, group_mean.rearrange("(k p) o -> p k o", p=P)).then_inc(xs_in, 16)
                    if dw and p == 0:
                        center(S, R, 2)
                    if dw and p == 3:
                        gelu(S, R, 0)
                    if Rg < NS:
                        evacuate_a(Sg, j, 0)
                    if dw and p == 0:
                        center(S, R, 1)
                    if dw and p == 3:
                        gelu(S, R, 2)
                    if Rg < NS:
                        evacuate_a(Sg, j, 1)
                    if p < NG - 2:
                        pair_x(S, R, p + 2)
                    else:
                        pair_x(S + 1, R + 1, p + 2 - NG)
                    if p > 0 and 1 <= R <= NS:
                        halo(S, R, p - 1)
                    if R == STRIPS - 1 and p == 2:
                        root(1)
                    if R < NS:
                        if R == STRIPS and p == 0:
                            act.wait_ge(beta_ready, 2)
                        evacuate_d(S, R, p)
                    if R >= 2 and (R < NS + 2 or p == 0):
                        evacuate_w(S, R, p)
                    if stats:
                        sum_chunk(S, R, p)

            pair_x(0, 0, 0)
            for h in range(2):
                evacuate_a(0, 0, h)
            pair_x(0, 0, 1)
            pipeline(act, step)

        @block.vector
        def _(dve):
            nc.vector.memset(gst[:], 0.0).then_inc(chunk_used, RING)
            nc.vector.memset(total[:], 0.0).then_inc(xs_used, 2)
            dve.wait_ge(set_in, 160)
            for k in range(KT):
                nc.vector.bn_stats(bnsamp[:, k], samp_s[:, k]).then_inc(reduced, 1)
            dve.wait_ge(reduced, KT)
            for k in range(KT):
                nc.vector.bn_aggr(sample[:, k], bnsamp[:, k]).then_inc(reduced, 1)
            dve.wait_ge(reduced, 2 * KT)
            nc.vector.tensor_scalar(shift[:], sample[:, :, 0], -1.0, None, ALU.mult).then_inc(reduced, 1)
            for k in range(KT):
                wait(dve, stat_ready, k)
                with dve.Fori(0, NCHUNK // RING) as i:
                    for r in range(RING):
                        dve.wait_ge(chunk_in[r], i * 16 + (k * (NCHUNK // RING) + 1) * 16)
                        for n in range(CHUNK // BN):
                            at = i * (RING * CHUNK // BN * 6) + (r * (CHUNK // BN) + n) * 6
                            ins = nc.vector.bn_stats(bnst[:, bass.ds(at, 6)],
                                                     acc[:, r].rearrange("p a b -> p (a b)")[:, n * BN:(n + 1) * BN])
                        ins.then_inc(chunk_used, 1)
                dve.wait_ge(chunk_used, RING + (k + 1) * NCHUNK)
                nc.vector.bn_aggr(mv[:, 0, k], bnst).then_inc(stat_ready, 1)
            dve.wait_ge(stat_ready, KT)
            dve.wait_ge(filter_made, 1)
            for q in range(2):
                nc.vector.tensor_copy(fil[:, q], ps[:, 7, 0:CH]).then_inc(fil_ready, 1)

            done = [0]

            def link(ins):
                done[0] += 1
                ins.then_inc(gs, 1)
                dve.wait_ge(gs, done[0])

            def group_stats(b, part, bank):
                v = [gst[:, b, n] for n in range(10)]
                mean, var = mv[:, b, :, 0], mv[:, b, :, 1]
                if part == 0:
                    link(nc.vector.tensor_copy(v[0], mean))
                if part == 1:
                    dve.wait_ge(gp, 3 * b + 1)
                    gm = ps[:, bank, 0:KT]
                    link(nc.vector.tensor_scalar(v[9], gm, -1.0, None, ALU.mult))
                    link(nc.vector.tensor_tensor(v[1], v[0], v[9], ALU.add))
                    link(nc.vector.tensor_tensor(v[2], v[1], v[1], ALU.mult))
                    link(nc.vector.tensor_tensor(v[3], v[2], var, ALU.add))
                if part == 2:
                    dve.wait_ge(gp, 3 * b + 2)
                    link(nc.vector.tensor_scalar(v[4], ps[:, bank, 0:KT], EPS, None, ALU.add))
                if part == 3:
                    dve.wait_ge(ga, b + 1)
                    link(nc.vector.reciprocal(v[6], v[5]))
                    link(nc.vector.tensor_tensor(v[7], v[6], v[6], ALU.mult))
                    link(nc.vector.tensor_tensor(v[8], v[7], v[4], ALU.mult))
                    link(nc.vector.tensor_scalar(v[7], v[8], -0.5, 1.5, ALU.mult, ALU.add))
                    link(nc.vector.tensor_tensor(v[8], v[6], v[7], ALU.mult))
                    for k in range(KT):
                        nc.vector.tensor_scalar(wi[:, b, k], wi[:, NB - 1, k], v[8][:, k:k + 1], None,
                                                ALU.mult).then_inc(wi_ready, 1)
                if part == 4:
                    dve.wait_ge(gp, 3 * b + 3)
                    nc.vector.tensor_tensor(beta[:, b], ps[:, bank, 0:KT], taps[:, :, 9], ALU.mult
                                            ).then_inc(beta_ready, 1)

            def sums_to_stats():
                n = [2 * KT + 1]

                def then(ins):
                    n[0] += 1
                    ins.then_inc(reduced, 1)
                    dve.wait_ge(reduced, n[0])

                dve.wait_ge(xs_used, 2 + 2 * NSUM)
                then(nc.vector.tensor_reduce(total[:], sums[:].rearrange("p a (k n) -> p a k n", k=KT),
                                             mybir.AxisListType.X, ALU.add))
                then(nc.vector.tensor_scalar(total[:], total[:], 1.0 / (H * W), None, ALU.mult))
                then(nc.vector.tensor_tensor(gst[:, 1, 7], total[:, 0], total[:, 0], ALU.mult))
                then(nc.vector.tensor_tensor(mv[:, 1, :, 1], total[:, 1], gst[:, 1, 7], ALU.subtract))
                then(nc.vector.tensor_tensor(mv[:, 1, :, 0], total[:, 0], shift[:], ALU.subtract))

            for part in range(5):
                group_stats(0, part, (None, 4, 5, None, 6)[part])
            dve.wait_ge(zeroed, 2)

            def stage_c(Sg, j, h):
                G = Sg * NG + j
                dve.wait_ge(b_done, G * 2 + (h + 1))
                wait(dve, d_done, G * KT - KT)
                nc.vector.tensor_tensor(tf[:, j % 2, h], ps[:, 2 * h:2 * h + 2, 0:CH], fil[:],
                                        ALU.mult).then_inc(tf_ready, 1)

            def window(S, R):
                w, w0 = S - 1, R - 1
                r = win_rows(w0)

                def first(k, op):
                    dst, src, wt = op
                    if w0 < NS:
                        dve.wait_ge(t_ready, S * (NG * KT))
                        wait(dve, halo_ready, w * KT)
                    if begins(w0) or w0 == NS:
                        wait(dve, edge_ready, w0 // STRIPS * KT)
                    wait(dve, g_ready, w * 2)
                    nc.vector.tensor_scalar(dst, src, wt, None, ALU.mult).then_inc(tap[k], 1)

                def other(k, n, op):
                    dst, src, wt = op
                    if n == 0:
                        if w0 == NS or begins(w0):
                            dve.wait_ge(center_ready[k], w + firsts(w0) + (1 if w0 == NS else 2))
                        else:
                            dve.wait_ge(center_ready[k], w + firsts(w0) + 1)
                    wait(dve, tap[k], taps_before(k, w, w0) + n)
                    nc.vector.scalar_tensor_tensor(dst, src, wt, dst, ALU.mult, ALU.add).then_inc(tap[k], 1)

                def product(k):
                    dve.wait_ge(gelu_ready, w * 2 + (1 if k == 0 else 2))
                    if k == 0:
                        dve.wait_ge(tap[1], taps_before(1, w + 1, w0 + 1))
                        a = acc[:, acc_of(1, w0), 0:r]
                        nc.vector.tensor_tensor(a, a, acc[:, ACC0, 0:r], ALU.mult).then_inc(g_ready, 1)
                    else:
                        a = acc[P - LO:P, acc_of(2, w0), 0:r]
                        nc.vector.tensor_tensor(a, a, gelu2(w0, r), ALU.mult).then_inc(g_ready, 1)

                todo = {}
                for k in range(KT):
                    centers, others = dw_ops(w0, k)
                    todo[k] = []
                    if k == 0:
                        todo[k] += [lambda k=k, o=o: first(k, o) for o in centers]
                    n0 = len(todo[k])
                    todo[k] += [lambda k=k, n=n, o=o, n0=n0: other(k, n + n0, o) for n, o in enumerate(others)]
                ops = []
                for n in range(max(len(todo[0]), len(todo[2]))):
                    for k in (0, 2):
                        ops += todo[k][n:n + 1]
                ops += todo[1][:5] + [lambda: product(2)] + todo[1][5:] + [lambda: product(0)]
                return ops

            def step(S, R):
                ops = window(S, R) if 1 <= R <= NS + 1 else []
                for p in range(NG):
                    mine = ops[len(ops) * p // NG:len(ops) * (p + 1) // NG]
                    Sg, Rg, j = (S, R, p + 1) if p < NG - 1 else (S + 1, R + 1, 0)
                    ahead = len(mine) * 4 // 7
                    if R == STRIPS - 1:
                        if p == 0:
                            sums_to_stats()
                            group_stats(1, 0, None)
                        else:
                            group_stats(1, (1, 2, 4)[p - 1], 4 + (2 * p) % 4)
                    for op in mine[:ahead]:
                        op()
                    if Rg < NS:
                        stage_c(Sg, j, 0)
                    for op in mine[ahead:ahead + 1]:
                        op()
                    if Rg < NS:
                        stage_c(Sg, j, 1)
                    if R == STRIPS - 1 and p == 2:
                        group_stats(1, 3, None)
                    for op in mine[ahead + 1:]:
                        op()

            for h in range(2):
                stage_c(0, 0, h)
            pipeline(dve, step)


def _constants(np):
    rows = np.arange(EDGE)
    basis, entries = [], []
    for k1 in range(EDGE):
        for k2 in range(EDGE // 2 + 1):
            angle = 2 * np.pi * (k1 * rows[:, None] + k2 * rows[None, :]) / EDGE
            k1n = (-k1) % EDGE
            own = k2 in (0, EDGE // 2)
            weight = np.zeros((EDGE, EDGE // 2 + 1))
            if own and k1 == k1n:
                weight[k1, k2] = 1.0
                basis.append(np.cos(angle) / EDGE)
                entries.append(weight)
            elif not own or k1 < k1n:
                weight[k1, k2] += 0.5 if own else 1.0
                if own:
                    weight[k1n, k2] += 0.5
                for f in (np.cos(angle), np.sin(angle)):
                    basis.append(f * np.sqrt(2.0) / EDGE)
                    entries.append(weight)
    basis = np.stack(basis)
    n = len(basis)
    dft = np.zeros((EDGE, 2, EDGE, 2, n))
    for patch in range(2):
        dft[:, patch, :, patch, :] = basis.transpose(1, 2, 0)
    dft = dft.reshape(P, P).astype(np.float32)
    entries = np.stack(entries).reshape(n, -1)
    select = np.concatenate([entries, entries]).T.astype(np.float32)
    group = np.arange(CH) // CPG
    group_mean = ((group[:, None] == group[None, :]) / CPG).astype(np.float32)
    return {"dft": dft, "dft_t": dft.T, "select": select, "group_mean": group_mean}


def kernel(x, L0_conv_fft_filter, L0_conv_w_in, L0_conv_w_dw, L0_conv_w_out):
    import numpy as np
    import concourse.bacc as bacc
    from concourse.bass_utils import run_bass_kernel_spmd as run

    order = np.concatenate([np.arange(P), HID2 + np.arange(P), np.arange(P, HID2), HID2 + np.arange(P, HID2)])
    w_in, w_dw, w_out = np.asarray(L0_conv_w_in), np.asarray(L0_conv_w_dw), np.asarray(L0_conv_w_out)
    fft = np.asarray(L0_conv_fft_filter)
    arrays = {
        "x": np.asarray(x),
        "w_in": w_in[order].T,
        "w_out": w_out.T,
        "w_dw": np.concatenate([w_dw[order].reshape(CH, 9), fft[order][:, 0, 0:1]], axis=1),
        "filt": fft[order].reshape(CH, -1).T,
        **_constants(np),
    }
    arrays = {f"in_{k}": np.ascontiguousarray(v) for k, v in arrays.items()}
    nc = bacc.Bacc("TRN2", target_bir_lowering=False, num_devices=1)
    args = [nc.dram_tensor(n, a.shape, mybir.dt.from_np(a.dtype), kind="ExternalInput").ap()
            for n, a in arrays.items()]
    out = nc.dram_tensor("out", (NB, CH, H, W), F32, kind="ExternalOutput").ap()
    conv_kernel(nc, *args, out)
    r = run(nc, [arrays], core_ids=[0])
    return r.results[0]["out"]
```

```python
from contextlib import ExitStack

import concourse.bass as bass
from concourse import mybir

F32 = mybir.dt.float32
F32R = mybir.dt.float32r
ALU = mybir.AluOpType
ACT = mybir.ActivationFunctionType

P = 128
EDGE = 8
NB, CH, H, W = 2, 384, 256, 256
KT = CH // P
GROUPS = 32
CPG = CH // GROUPS
EPS = 1e-5
STRIPS = H // EDGE
NS = NB * STRIPS
GC = 64
NG = W // GC
PC = 16
NPAIR = GC // PC
HC = W // 2
TW = W + 2
WIN = EDGE * W
BN = 512
CHUNK = WIN
NCHUNK = H * W // CHUNK
RING = 4
FIRST = 3
PER_TILE = NCHUNK // NG
NSUM = KT * NCHUNK
HID2 = CH // 2
LO = HID2 - P

SPLIT = 1
WHOLE = KT - SPLIT
GSTEPS = 11

ACC0, ACC1, ACC2, NACC = 0, (1, 2), (3, 3), 4


def acc_of(tile, w):
    return ACC0 if tile == 0 else (ACC1, ACC2)[tile - 1][w % 2]


def begins(w):
    return w < NS and w % STRIPS == 0


def firsts(w):
    return (w + STRIPS - 1) // STRIPS if w < NS else NB


def n_taps(tile, w):
    per = 7 if tile else 8
    edge_taps = 5 if tile else 6
    return edge_taps if w == NS else per + (edge_taps if begins(w) else 0)


def taps_before(tile, w, w0):
    if w0 == NS + 1:
        return taps_before(tile, NS, NS) + n_taps(tile, NS)
    return w * n_taps(tile, 1) + firsts(w0) * (n_taps(tile, 0) - n_taps(tile, 1))


def stores_before(w, w0):
    return w + sum(1 for b in range(1, NB) if w0 > b * STRIPS)


def conv_kernel(nc, x, w_in, w_out, w_dw, filt, dft, dft_t, select, group_mean, out):
    xc = x.rearrange("b (k p) h w -> (b k) p (h w)", p=P)
    orow = out.rearrange("b (k p) h w -> (b k) p h w", p=P)
    xr = x.rearrange("b (k p) h w -> (b k) p h w", p=P)

    with ExitStack() as ctx:
        def sb(name, shape, dt=F32):
            return ctx.enter_context(nc.sbuf_tensor(name, shape, dt))

        def sem(name):
            return ctx.enter_context(nc.semaphore(name))

        t_buf = sb("t_buf", [P, 2, KT, EDGE + 2, TW])
        acc = sb("acc", [P, NACC, EDGE, W])
        y = sb("y", [P, 2, EDGE, W])
        xh = sb("xh", [P, 2, KT, EDGE, HC])
        xp = sb("xp", [P, WHOLE, NPAIR, EDGE * PC])
        xp_hi = sb("xp_hi", [P, SPLIT, NPAIR, EDGE * PC], F32R)
        xp_lo = sb("xp_lo", [P, SPLIT, NPAIR, EDGE * PC], F32R)
        tmp = sb("tmp", [P, EDGE, W])
        g2 = sb("g2", [P, EDGE, W], F32R)
        pool_s = sb("pool_s", [P, 2])
        xs = sb("xs", [P, CHUNK])
        ta = sb("ta", [P, 2, 2, CH])
        tf = sb("tf", [P, 2, 2, 2, CH])
        w_raw = sb("w_raw", [P, KT, CH])
        wi0 = sb("wi0", [P, WHOLE, CH])
        wi_hi = sb("wi_hi", [P, SPLIT, CH], F32R)
        wi_lo = sb("wi_lo", [P, SPLIT, CH], F32R)
        wo = sb("wo", [P, CH])
        wo_hi = sb("wo_hi", [P, CH], F32R)
        wo_lo = sb("wo_lo", [P, CH], F32R)
        fil = sb("fil", [P, 1, CH])
        dft_s = sb("dft_s", [P, P])
        dftt_s = sb("dftt_s", [P, P])
        taps = sb("taps", [P, KT, 10])
        beta = sb("beta", [P, NB, KT])
        mv = sb("mv", [P, NB, KT, 2])
        gst = sb("gst", [P, NB, 10, KT])
        sample = sb("sample", [P, KT, 2])
        shift = sb("shift", [P, KT])
        sums = sb("sums", [P, 2, NSUM])
        total = sb("total", [P, 2, KT])
        edge = xs[:, 0:KT * 2 * TW].rearrange("p (k r c) -> p k r c", k=KT, r=2)
        gmean_s = xs[:, 0:KT * CH].rearrange("p (k c) -> p k c", k=KT)
        y0 = y[:, 0].rearrange("p a b -> p (a b)")
        y1 = y[:, 1].rearrange("p a b -> p (a b)")
        bnst = y0[:, 0:NCHUNK * (CHUNK // BN) * 6]
        sel_s = y1[0:40, 0:P]
        filt_s = y1[0:40, P:P + CH]
        wo_raw = y1[:, 1024:1024 + CH]
        wi0_s = tmp[:].rearrange("p a b -> p (a b)")[:, 0:SPLIT * CH].rearrange("p (k c) -> p k c", k=SPLIT)
        bnsamp = y1[:, P + CH:P + CH + 6 * KT].rearrange("p (k n) -> p k n", k=KT)
        samp_s = tmp[:].rearrange("p a b -> p (a b)")[:, 0:KT * BN].rearrange("p (k n) -> p k n", k=KT)

        ps = ctx.enter_context(nc.psum_tensor("ps", [P, 8, 512], F32))

        set_in = sem("set_in")
        chunk_in = [sem(f"chunk_in{r}") for r in range(RING)]
        chunk_used = sem("chunk_used")
        xs_in = sem("xs_in")
        xs_used = sem("xs_used")
        reduced = sem("reduced")
        stat_ready = sem("stat_ready")
        gs = sem("gs")
        filter_made = sem("filter_made")
        fil_ready = sem("fil_ready")
        gp = sem("gp")
        ga = sem("ga")
        wi_ready = sem("wi_ready")
        beta_ready = sem("beta_ready")
        zeroed = sem("zeroed")
        edge_ready = sem("edge_ready")
        x_in = [sem("x_in0"), sem("x_in1")]
        xp_ready = sem("xp_ready")
        lo_ready = sem("lo_ready")
        wi_split = sem("wi_split")
        a_done = sem("a_done")
        ta_ready = sem("ta_ready")
        b_done = sem("b_done")
        tf_ready = sem("tf_ready")
        d_done = sem("d_done")
        t_ready = sem("t_ready")
        halo_ready = sem("halo_ready")
        wo_split = sem("wo_split")
        tmp_ready = sem("tmp_ready")
        tap_in = [sem(f"tap_in{k}") for k in range(KT)]
        pool_step = sem("pool_step")
        g2_ready = sem("g2_ready")
        center_ready = [sem(f"center_ready{k}") for k in range(KT)]
        tap = [sem(f"tap{k}") for k in range(KT)]
        gelu_ready = sem("gelu_ready")
        g_ready = sem("g_ready")
        w_done = sem("w_done")
        y_ready = sem("y_ready")
        res_in = [sem(f"res_in{m}") for m in range(KT)]
        stored = [sem(f"stored{m}") for m in range(KT)]

        def wait(eng, s, value):
            if not isinstance(value, int) or value > 0:
                eng.wait_ge(s, value)

        def wi(b, k):
            return w_raw[:, k] if b == NB - 1 else wi0[:, k] if k < WHOLE else wi0_s[:, k - WHOLE]

        def pipeline(eng, step):
            def loop(first, n):
                if n:
                    with eng.Fori(0, n // 2) as i:
                        for u in (first, first + 1):
                            step(i * 2 + u, u)

            for b in range(NB):
                s0 = b * STRIPS
                for S in range(s0, s0 + FIRST):
                    step(S, S)
                if b == 0:
                    for k in range(KT):
                        loop(FIRST + k * PER_TILE, PER_TILE)
                    loop(FIRST + KT * PER_TILE, STRIPS - 1 - FIRST - KT * PER_TILE)
                else:
                    loop(s0 + FIRST, STRIPS - 1 - FIRST)
                step(s0 + STRIPS - 1, s0 + STRIPS - 1)
            for S in range(NS, NS + 3):
                step(S, S)

        def dw_rows(w0, k):
            par = w0 % 2
            whole = (0, EDGE, lambda di, r: t_buf[:, par, k, 1 + di + r:1 + di + r + EDGE], (-1, 0, 1))
            if w0 == NS:
                return [(0, 1, lambda di, r: edge[:, k, 1 + di:2 + di], (-1, 0))]
            if begins(w0):
                return [(1, EDGE - 1, lambda di, r: t_buf[:, par, k, 2 + di:1 + di + EDGE], (-1, 0, 1)),
                        (0, 1, lambda di, r: edge[:, k, 1 + di:2 + di], (-1, 0))]
            return [whole]

        def dw_ops(w0, k):
            centers, by_dma, others = [], [], []
            for r0, nr, source, dis in dw_rows(w0, k):
                for di in dis:
                    for dj in (-1, 0, 1):
                        op = (acc[:, acc_of(k, w0), r0:r0 + nr], source(di, 0)[:, :, 1 + dj:1 + dj + W],
                              taps[:, k, (di + 1) * 3 + dj + 1:(di + 1) * 3 + dj + 2])
                        main = nr > 1 and (di, dj) == (0, 1)
                        (centers if (di, dj) == (0, 0) else by_dma if main else others).append(op)
            return centers, by_dma, others

        def tmp_rows(w0):
            return tmp[:, 1:EDGE] if begins(w0) else tmp[:]

        def paired(k, j):
            return xh[:, j // 2, k, :, (j % 2) * GC:(j % 2 + 1) * GC].rearrange("p r (q c) -> p q r c", c=PC)

        def gelu2(w0, rows):
            return t_buf[P - LO:P, w0 % 2, 2, 0:rows, 1:1 + W]

        def y_parts(w, w0):
            b = min(w0 // STRIPS, NB - 1)
            if w0 < NS and not begins(w0):
                return [(b, (w - b * STRIPS) * EDGE - 1, 0, EDGE)]
            parts = [(b, 0, 1, EDGE - 1)] if w0 < NS else []
            return parts + [((w0 - 1) // STRIPS, H - 1, 0, 1)] * (w0 > 0)

        def win_rows(w0):
            return 1 if w0 == NS else EDGE

        block = ctx.enter_context(nc.Block())

        @block.sync
        def _(sp):
            for dst, src in ((w_raw[:], w_in.rearrange("(k p) o -> p k o", p=P)),
                             (gmean_s, group_mean.rearrange("(k p) o -> p k o", p=P)),
                             (wo[:], w_out[0:P]),
                             (wo_raw[0:LO], w_out[P:HID2]),
                             (wo_raw[P - LO:P], w_out[P:HID2]),
                             (dft_s[:], dft), (dftt_s[:], dft_t), (sel_s, select), (filt_s, filt),
                             (taps[:], w_dw.rearrange("(k p) o -> p k o", p=P)),
                             (samp_s, xc[KT:2 * KT, :, 0:BN].rearrange("k p n -> p k n"))):
                sp.dma_start(dst, src).then_inc(set_in, 16)
            for k in range(KT):
                with sp.Fori(0, NCHUNK // RING) as i:
                    for r in range(RING):
                        sp.wait_ge(chunk_used, i * RING + (k * NCHUNK + r + 1))
                        sp.dma_start(acc[:, r].rearrange("p a b -> p (a b)"),
                                     xc[k, :, bass.ds(i * (RING * CHUNK) + r * CHUNK, CHUNK)]
                                     ).then_inc(chunk_in[r], 16)

            def store(S, R):
                w, w0 = S - 2, R - 2
                if w0 < 0:
                    return
                for m in range(KT):
                    parts = y_parts(w, w0)
                    sp.wait_ge(res_in[m], (stores_before(w, w0) + len(parts)) * 16)
                    for b, top, r0, nr in parts:
                        sp.dma_start(orow[b * KT + m, :, bass.ds(top, nr)], y[:, (w0 + m) % 2, r0:r0 + nr]
                                     ).then_inc(stored[m], 16)

            pipeline(sp, store)
            for m in range(KT):
                sp.wait_ge(stored[m], 16 * stores_before(NS + 1, NS + 1))

        @block.gpsimd
        def _(pool):
            nc.gpsimd.memset(t_buf[:], 0.0).then_inc(zeroed, 1)
            pool.wait_ge(gp, 2)
            nc.gpsimd.memset(edge, 0.0).then_inc(zeroed, 1)
            nc.gpsimd.memset(pool_s[:], 0.0).then_inc(pool_step, 1)
            pool.wait_ge(pool_step, 1)

            def add_x(S, R, m):
                w, w0 = S - 2, R - 2
                if w0 < 0:
                    return
                pool.wait_ge(y_ready, w * (KT * NG) + (m + 1) * (1 if w0 == NS else NG))
                for b, top, r0, nr in y_parts(w, w0):
                    pool.dma_start(y[:, (w0 + m) % 2, r0:r0 + nr], xr[b * KT + m, :, bass.ds(top, nr)],
                                   accum_op=ALU.add).then_inc(res_in[m], 16)

            def add_tap(S, R, n, k):
                w, w0 = S - 1, R - 1
                if not 0 <= w0 < NS:
                    return
                if k:
                    pool.wait_ge(center_ready[k], w + firsts(w0) + (2 if begins(w0) else 1))
                else:
                    pool.wait_ge(tap[0], taps_before(0, w + 1, w0 + 1))
                pool.wait_ge(pool_step, w * KT + (n + 1))
                pool.wait_ge(tmp_ready, w * KT + (n + 1))
                nc.gpsimd.tensor_tensor(pool_s[:, 1:2], pool_s[:, 0:1], pool_s[:, 0:1], ALU.add).then_inc(pool_step, 1)
                pool.dma_start(dw_ops(w0, k)[1][0][0], tmp_rows(w0), accum_op=ALU.add).then_inc(tap_in[k], 16)

            def step(S, R):
                add_tap(S, R, 0, 2)
                add_tap(S, R, 1, 1)
                add_x(S, R, 0)
                add_tap(S, R, 2, 0)
                add_x(S, R, 1)
                add_x(S, R, 2)

            pipeline(pool, step)

        @block.tensor
        def _(pe):
            pe.wait_ge(set_in, 176)
            nc.tensor.matmul(ps[:, 7, 0:CH], sel_s, filt_s, start=True, stop=True).then_inc(filter_made, 1)

            def small(b, n, bank):
                if n < 2:
                    pe.wait_ge(gs, b * GSTEPS + (1, 5)[n])
                else:
                    pe.wait_ge(wi_ready, (b + 1) * KT)
                for k in range(KT):
                    for c in range(KT):
                        lhs = (gmean_s[:, c] if n < 2 else wi(b, c))[:, k * P:(k + 1) * P]
                        mm = nc.tensor.matmul(ps[:, bank, k:k + 1], lhs, gst[:, b, (0, 3, 9)[n], c:c + 1],
                                              start=(c == 0), stop=(c == KT - 1))
                mm.then_inc(gp, 1)

            for n in range(3):
                small(0, n, 4 + n)

            def stage_a(Sg, Rg0, j, h):
                G = Sg * NG + j
                b = Rg0 // STRIPS
                if h == 0:
                    pe.wait_ge(xp_ready, G * KT + KT)
                    pe.wait_ge(lo_ready, G * SPLIT + SPLIT)
                if h == 0 and j == 0 and Rg0 % STRIPS == 0:
                    pe.wait_ge(wi_split, (b + 1) * 2 * SPLIT)
                wait(pe, tf_ready, G * 2 + (h - 1))
                for q in range(2):
                    o = ps[:, 2 * h + q, 0:CH]
                    for k in range(WHOLE):
                        mm = nc.tensor.matmul(o, xp[:, k, 2 * h + q], wi(b, k), start=(k == 0),
                                              stop=(k == KT - 1))
                    for k in range(SPLIT):
                        hi, lo = xp_hi[:, k, 2 * h + q], xp_lo[:, k, 2 * h + q]
                        nc.tensor.matmul(o, hi, wi_hi[:, k], start=(WHOLE + k == 0), stop=False)
                        nc.tensor.matmul(o, hi, wi_lo[:, k], start=False, stop=False)
                        mm = nc.tensor.matmul(o, lo, wi_hi[:, k], start=False, stop=(k == SPLIT - 1))
                mm.then_inc(a_done, 1)

            def stage_b(Sg, j, h):
                pe.wait_ge(ta_ready, (Sg * NG + j) * 2 + (h + 1))
                for q in range(2):
                    mm = nc.tensor.matmul(ps[:, 2 * h + q, 0:CH], dft_s[:], ta[:, h, q, :], start=True, stop=True)
                mm.then_inc(b_done, 1)

            def stage_d(S, R, p):
                G, G0 = S * NG + p, R * NG + p
                pe.wait_ge(tf_ready, G * 2 + 2)
                if G0 == 0:
                    pe.wait_ge(beta_ready, 1)
                    pe.wait_ge(fil_ready, 1)
                if R == STRIPS - 1 and p > 0:
                    pe.wait_ge((gs, gs, beta_ready)[p - 1], (GSTEPS + 2, GSTEPS + 6, 2)[p - 1])
                for k in range(KT):
                    if k == 0:
                        wait(pe, t_ready, G * KT)
                    elif G0 > 2 * NG:
                        pe.wait_ge(y_ready, G * KT - (2 * NG + 1) * KT + k)
                    bank = ps[:, 4 + (2 * p + k) % 4].rearrange("p (r c) -> p r c", c=GC)
                    for q in range(NPAIR):
                        mm = nc.tensor.matmul(bank[:, :, q * PC:(q + 1) * PC],
                                              tf[:, p % 2, q // 2, q % 2, k * P:(k + 1) * P], dftt_s[:],
                                              start=True, stop=True)
                    mm.then_inc(d_done, 1)

            def stage_w(S, R, p):
                w, w0 = S - 2, R - 2
                G = S * NG + p
                rows = win_rows(w0)
                cols = W if w0 == NS else GC
                if p == 0:
                    pe.wait_ge(g_ready, w * 2 + 2)
                    pe.wait_ge(g2_ready, w * 2 + 2)
                for i in range(KT):
                    u = KT * p + i
                    m, n = (i, 0) if w0 == NS else (u // NG, u % NG)
                    if i == 0:
                        wait(pe, y_ready, G * KT - 2 * NG * KT)
                    elif R < NS:
                        pe.wait_ge(t_ready, G * KT + i)
                    o = ps[:, 4 + (2 * p + 3 + i) % 4, 0:rows * cols].rearrange("p (r c) -> p r c", c=cols)
                    mw = slice(m * P, (m + 1) * P)
                    nw = slice(n * GC, n * GC + cols)
                    nc.tensor.matmul(o, wo[:, mw], acc[:, acc_of(1, w0), 0:rows, nw], start=True, stop=False)
                    nc.tensor.matmul(o, wo_hi[:, mw], g2[:, 0:rows, nw], start=False, stop=False)
                    nc.tensor.matmul(o, wo_lo[P - LO:P, mw], g2[P - LO:P, 0:rows, nw],
                                     start=False, stop=True).then_inc(w_done, 1)

            def step(S, R):
                for p in range(NG):
                    Sg, Rg, j = (S, R, p + 1) if p < NG - 1 else (S + 1, R + 1, 0)
                    if R == STRIPS - 1 and p > 0:
                        if p == 1:
                            pe.wait_ge(xs_in, 16 * (NSUM + 1))
                        pe.wait_ge(t_ready, (S * NG + p) * KT)
                        small(1, p - 1, 4 + (2 * p) % 4)
                    if Rg < NS:
                        for h in range(2):
                            stage_a(Sg, Rg, j, h)
                        for h in range(2):
                            stage_b(Sg, j, h)
                    if R < NS:
                        stage_d(S, R, p)
                    elif p == 0 and R == NS:
                        pe.wait_ge(t_ready, NS * NG * KT)
                    if R >= 2 and (R < NS + 2 or p == 0):
                        stage_w(S, R, p)

            pe.wait_ge(wo_split, 2)
            for h in range(2):
                stage_a(0, 0, 0, h)
            for h in range(2):
                stage_b(0, 0, h)
            pipeline(pe, step)

        @block.scalar
        def _(act):
            def load(Sg, Rg, h):
                if Rg >= NS:
                    return
                if Rg > 0:
                    act.wait_ge(xp_ready, Sg * (NG * KT) + (h - 1) * (NG * KT // 2))
                    act.wait_ge(lo_ready, (Sg * (NG * SPLIT) + (h - 1) * (NG * SPLIT // 2)))
                b = Rg // STRIPS
                for k in range(KT):
                    act.dma_start(xh[:, h, k], xr[b * KT + k, :, bass.ds((Sg - b * STRIPS) * EDGE, EDGE),
                                                  h * HC:(h + 1) * HC]).then_inc(x_in[h], 16)

            for h in range(2):
                load(0, 0, h)
            def root(b):
                act.wait_ge(gs, b * GSTEPS + 6)
                nc.scalar.activation(gst[:, b, 5], gst[:, b, 4], ACT.Sqrt).then_inc(ga, 1)

            root(0)
            act.wait_ge(zeroed, 2)
            act.wait_ge(beta_ready, 1)

            def load_chunk(S, R, p):
                n, k = (S - FIRST) * NG + p, (R - FIRST) // PER_TILE
                if R == FIRST and p == 0:
                    for t in range(KT):
                        act.wait_ge(tap[t], taps_before(t, 1, 1))
                act.wait_ge(xs_used, n * 2 + 2)
                act.dma_start(xs[:], xc[KT + k, :, bass.ds(n * CHUNK - k * (NCHUNK * CHUNK), CHUNK)]
                              ).then_inc(xs_in, 16)

            def sum_chunk(S, R, p):
                n, k = (S - FIRST) * NG + p, (R - FIRST) // PER_TILE
                act.wait_ge(xs_in, n * 16 + 16)
                nc.scalar.activation(xs[:], xs[:], ACT.Identity, bias=shift[:, k:k + 1],
                                     accum_out=sums[:, 0, bass.ds(n, 1)]).then_inc(xs_used, 1)

            def sum_squares(S, R, p):
                n, k = (S - FIRST) * NG + p, (R - FIRST) // PER_TILE
                act.wait_ge(xs_used, n * 2 + 3)
                nc.scalar.activation(xs[:], xs[:], ACT.Square,
                                     accum_out=sums[:, 1, bass.ds(n, 1)]).then_inc(xs_used, 1)

            def pair_x(Sg, Rg, j):
                if Rg >= NS:
                    return
                if j % 2 == 0:
                    act.wait_ge(x_in[j // 2], Sg * (16 * KT) + 16 * KT)
                wait(act, a_done, (Sg * NG + j) * 2)
                for k in range(KT):
                    dst = xp[:, k] if k < WHOLE else xp_hi[:, k - WHOLE]
                    nc.scalar.activation(dst.rearrange("p q (r c) -> p q r c", c=PC), paired(k, j),
                                         ACT.Identity).then_inc(xp_ready, 1)

            def evacuate_a(Sg, j, h):
                G = Sg * NG + j
                act.wait_ge(a_done, G * 2 + (h + 1))
                wait(act, b_done, G * 2 + (h - 1))
                nc.scalar.activation(ta[:, h], ps[:, 2 * h:2 * h + 2, 0:CH], ACT.Identity).then_inc(ta_ready, 1)

            def evacuate_d(S, R, p):
                for k in range(KT):
                    act.wait_ge(d_done, (S * NG + p) * KT + (k + 1))
                    if p == 0 and R > 1:
                        act.wait_ge(tap[k], taps_before(k, S - 1, R - 1))
                        if k == 2:
                            act.wait_ge(g_ready, S * 2 - 3)
                    nc.scalar.activation(t_buf[:, R % 2, k, 2:2 + EDGE, 1 + p * GC:1 + (p + 1) * GC],
                                         ps[:, 4 + (2 * p + k) % 4].rearrange("p (r c) -> p r c", c=GC),
                                         ACT.Identity, bias=beta[:, R // STRIPS, k:k + 1]).then_inc(t_ready, 1)

            def evacuate_w(S, R, p):
                w, w0 = S - 2, R - 2
                rows = win_rows(w0)
                cols = W if w0 == NS else GC
                for i in range(KT):
                    u = KT * p + i
                    m, n = (i, 0) if w0 == NS else (u // NG, u % NG)
                    act.wait_ge(w_done, (S * NG + p) * KT - 2 * NG * KT + (i + 1))
                    if n == 0 and m == 2:
                        act.wait_ge(stored[0], (stores_before(w, w0) + len(y_parts(w, w0))) * 16)
                    elif n == 0 and w0 > 0:
                        act.wait_ge(stored[m + 1], stores_before(w, w0) * 16)
                    nc.scalar.activation(y[:, (w0 + m) % 2, 0:rows, n * GC:n * GC + cols],
                                         ps[:, 4 + (2 * p + 3 + i) % 4, 0:rows * cols
                                            ].rearrange("p (r c) -> p r c", c=cols),
                                         ACT.Identity).then_inc(y_ready, 1)

            def halo(S, R, k):
                last_rows = t_buf[:, (R - 1) % 2, k, EDGE:EDGE + 2]
                act.wait_ge(t_ready, S * (NG * KT))
                if R > 1:
                    act.wait_ge(tap[k], taps_before(k, S - 1, R - 1))
                if R % STRIPS == 0:
                    act.wait_ge(gp, 3 + 2)
                    nc.scalar.activation(edge[:, k], last_rows, ACT.Identity).then_inc(edge_ready, 1)
                    last_rows = t_buf[:, (R - 1) % 2, k, EDGE:EDGE + 2, 0:1].to_broadcast([P, 2, TW])
                if R < NS:
                    nc.scalar.activation(t_buf[:, R % 2, k, 0:2], last_rows, ACT.Identity).then_inc(halo_ready, 1)

            def center(S, R, k):
                w, w0 = S - 1, R - 1
                act.wait_ge(t_ready, min(R, NS) * (NG * KT) if R >= NS else S * (NG * KT))
                wait(act, halo_ready, (min(w0, NS - 1) if w0 >= NS - 1 else w) * KT)
                if begins(w0) or w0 == NS:
                    wait(act, edge_ready, w0 // STRIPS * KT)
                if k == 1 and w0 >= 2:
                    act.wait_ge(w_done, (w - 1) * (KT * NG))
                if k == 2:
                    wait(act, g2_ready, w * 2)
                ops = dw_ops(w0, k)[0]
                for n, (a, src, wt) in enumerate(ops):
                    nc.scalar.activation(a, src, ACT.Copy, scale=wt).then_inc(center_ready[k], 1)

            def product(S, R, k):
                w, w0 = S - 1, R - 1
                if w0 == NS:
                    return
                wait(act, tap_in[(k + 1) % KT], w * 16 + (0 if k == 2 else 16))
                _, src, wt = dw_ops(w0, k)[1][0]
                nc.scalar.activation(tmp_rows(w0), src, ACT.Copy, scale=wt).then_inc(tmp_ready, 1)

            def leading_part(S, R):
                w, w0 = S - 2, R - 2
                act.wait_ge(g_ready, w * 2 + 1)
                wait(act, w_done, w * (KT * NG))
                r = win_rows(w0)
                nc.scalar.activation(g2[P - LO:P, 0:r], acc[P - LO:P, acc_of(2, w0), 0:r],
                                     ACT.Identity).then_inc(g2_ready, 1)

            def gelu(S, R, k):
                w, w0 = S - 1, R - 1
                r = win_rows(w0)
                if k == 0 and w0 < NS:
                    act.wait_ge(tap_in[0], w * 16 + 16)
                else:
                    act.wait_ge(tap[k], taps_before(k, w + 1, w0 + 1))
                if k == 0:
                    nc.scalar.activation(acc[:, ACC0, 0:r], acc[:, ACC0, 0:r], ACT.Gelu).then_inc(gelu_ready, 1)
                else:
                    nc.scalar.activation(gelu2(w0, r), acc[0:LO, acc_of(2, w0), 0:r],
                                         ACT.Gelu).then_inc(gelu_ready, 1)

            def step(S, R):
                for p in range(NG):
                    Sg, Rg, j = (S, R, p + 1) if p < NG - 1 else (S + 1, R + 1, 0)
                    dw = 1 <= R <= NS + 1
                    if p % 2 == 0:
                        load(S + 1, R + 1, p // 2)
                    stats = FIRST <= R < FIRST + KT * PER_TILE
                    if stats:
                        load_chunk(S, R, p)
                    if R == STRIPS - 1 and p == 0:
                        act.wait_ge(xs_used, 2 + 2 * NSUM)
                        act.dma_start(gmean_s, group_mean.rearrange("(k p) o -> p k o", p=P)).then_inc(xs_in, 16)
                    if p == 0 and R >= 2:
                        leading_part(S, R)
                    if dw and p == 3:
                        gelu(S, R, 2)
                    if Rg < NS:
                        evacuate_a(Sg, j, 0)
                    if dw and p < 2:
                        center(S, R, 2 - p)
                    if Rg < NS:
                        evacuate_a(Sg, j, 1)
                    if dw and p == 3:
                        gelu(S, R, 0)
                    if dw and p < 3:
                        product(S, R, 2 - p)
                    if p < NG - 2:
                        pair_x(S, R, p + 2)
                    else:
                        pair_x(S + 1, R + 1, p + 2 - NG)
                    if p > 0 and 1 <= R <= NS:
                        halo(S, R, p - 1)
                    if R == STRIPS - 1 and p == 2:
                        root(1)
                    if R < NS:
                        if R == STRIPS and p == 0:
                            act.wait_ge(beta_ready, 2)
                        evacuate_d(S, R, p)
                    if stats:
                        sum_chunk(S, R, p)
                    if R >= 2 and (R < NS + 2 or p == 0):
                        evacuate_w(S, R, p)
                    if stats:
                        sum_squares(S, R, p)

            pair_x(0, 0, 0)
            for h in range(2):
                evacuate_a(0, 0, h)
            pair_x(0, 0, 1)
            pipeline(act, step)

        @block.vector
        def _(dve):
            nc.vector.memset(gst[:], 0.0).then_inc(chunk_used, RING)
            nc.vector.memset(total[:], 0.0).then_inc(xs_used, 2)
            dve.wait_ge(set_in, 176)
            for k in range(KT):
                nc.vector.bn_stats(bnsamp[:, k], samp_s[:, k]).then_inc(reduced, 1)
            dve.wait_ge(reduced, KT)
            for k in range(KT):
                nc.vector.bn_aggr(sample[:, k], bnsamp[:, k]).then_inc(reduced, 1)
            dve.wait_ge(reduced, 2 * KT)
            nc.vector.tensor_scalar(shift[:], sample[:, :, 0], -1.0, None, ALU.mult).then_inc(reduced, 1)
            for k in range(KT):
                wait(dve, stat_ready, k)
                with dve.Fori(0, NCHUNK // RING) as i:
                    for r in range(RING):
                        dve.wait_ge(chunk_in[r], i * 16 + (k * (NCHUNK // RING) + 1) * 16)
                        for n in range(CHUNK // BN):
                            at = i * (RING * CHUNK // BN * 6) + (r * (CHUNK // BN) + n) * 6
                            ins = nc.vector.bn_stats(bnst[:, bass.ds(at, 6)],
                                                     acc[:, r].rearrange("p a b -> p (a b)")[:, n * BN:(n + 1) * BN])
                        ins.then_inc(chunk_used, 1)
                dve.wait_ge(chunk_used, RING + (k + 1) * NCHUNK)
                nc.vector.bn_aggr(mv[:, 0, k], bnst).then_inc(stat_ready, 1)
            dve.wait_ge(stat_ready, KT)
            nc.vector.tensor_copy(wo_hi[:], wo_raw).then_inc(wo_split, 1)
            dve.wait_ge(wo_split, 1)
            nc.vector.tensor_tensor(wo_lo[:], wo_raw, wo_hi[:].bitcast(F32), ALU.subtract).then_inc(wo_split, 1)
            dve.wait_ge(filter_made, 1)
            nc.vector.tensor_copy(fil[:, 0], ps[:, 7, 0:CH]).then_inc(fil_ready, 1)

            done = [0]

            def link(ins):
                done[0] += 1
                ins.then_inc(gs, 1)
                dve.wait_ge(gs, done[0])

            def group_stats(b, part, bank):
                v = [gst[:, b, n] for n in range(10)]
                mean, var = mv[:, b, :, 0], mv[:, b, :, 1]
                if part == 0:
                    link(nc.vector.tensor_copy(v[0], mean))
                if part == 1:
                    dve.wait_ge(gp, 3 * b + 1)
                    gm = ps[:, bank, 0:KT]
                    link(nc.vector.tensor_scalar(v[9], gm, -1.0, None, ALU.mult))
                    link(nc.vector.tensor_tensor(v[1], v[0], v[9], ALU.add))
                    link(nc.vector.tensor_tensor(v[2], v[1], v[1], ALU.mult))
                    link(nc.vector.tensor_tensor(v[3], v[2], var, ALU.add))
                if part == 2:
                    dve.wait_ge(gp, 3 * b + 2)
                    link(nc.vector.tensor_scalar(v[4], ps[:, bank, 0:KT], EPS, None, ALU.add))
                if part == 3:
                    dve.wait_ge(ga, b + 1)
                    link(nc.vector.reciprocal(v[6], v[5]))
                    link(nc.vector.tensor_tensor(v[7], v[6], v[6], ALU.mult))
                    link(nc.vector.tensor_tensor(v[8], v[7], v[4], ALU.mult))
                    link(nc.vector.tensor_scalar(v[7], v[8], -0.5, 1.5, ALU.mult, ALU.add))
                    link(nc.vector.tensor_tensor(v[8], v[6], v[7], ALU.mult))
                    for k in range(KT):
                        nc.vector.tensor_scalar(wi(b, k), w_raw[:, k], v[8][:, k:k + 1], None,
                                                ALU.mult).then_inc(wi_ready, 1)
                    dve.wait_ge(wi_ready, (b + 1) * KT)
                    if b > 0:
                        dve.wait_ge(a_done, b * STRIPS * NG * 2)
                    for k in range(SPLIT):
                        nc.vector.tensor_copy(wi_hi[:, k], wi(b, WHOLE + k)).then_inc(wi_split, 1)
                    dve.wait_ge(wi_split, (2 * b + 1) * SPLIT)
                    for k in range(SPLIT):
                        nc.vector.tensor_tensor(wi_lo[:, k], wi(b, WHOLE + k), wi_hi[:, k].bitcast(F32),
                                                ALU.subtract).then_inc(wi_split, 1)
                if part == 4:
                    dve.wait_ge(gp, 3 * b + 3)
                    nc.vector.tensor_tensor(beta[:, b], ps[:, bank, 0:KT], taps[:, :, 9], ALU.mult
                                            ).then_inc(beta_ready, 1)

            def sums_to_stats():
                n = [2 * KT + 1]

                def then(ins):
                    n[0] += 1
                    ins.then_inc(reduced, 1)
                    dve.wait_ge(reduced, n[0])

                dve.wait_ge(xs_used, 2 + 2 * NSUM)
                then(nc.vector.tensor_reduce(total[:], sums[:].rearrange("p a (k n) -> p a k n", k=KT),
                                             mybir.AxisListType.X, ALU.add))
                then(nc.vector.tensor_scalar(total[:], total[:], 1.0 / (H * W), None, ALU.mult))
                then(nc.vector.tensor_tensor(gst[:, 1, 7], total[:, 0], total[:, 0], ALU.mult))
                then(nc.vector.tensor_tensor(mv[:, 1, :, 1], total[:, 1], gst[:, 1, 7], ALU.subtract))
                then(nc.vector.tensor_tensor(mv[:, 1, :, 0], total[:, 0], shift[:], ALU.subtract))

            for part in range(5):
                group_stats(0, part, (None, 4, 5, None, 6)[part])
            dve.wait_ge(zeroed, 2)

            def rest_of_x(Sg, Rg, j):
                if Rg >= NS:
                    return
                dve.wait_ge(xp_ready, (Sg * NG + j) * KT + KT)
                for k in range(SPLIT):
                    nc.vector.tensor_tensor(xp_lo[:, k].rearrange("p q (r c) -> p q r c", c=PC),
                                            paired(WHOLE + k, j),
                                            xp_hi[:, k].bitcast(F32).rearrange("p q (r c) -> p q r c", c=PC),
                                            ALU.subtract).then_inc(lo_ready, 1)

            def stage_c(Sg, j, h):
                G = Sg * NG + j
                dve.wait_ge(b_done, G * 2 + (h + 1))
                wait(dve, d_done, G * KT - KT)
                nc.vector.tensor_tensor(tf[:, j % 2, h], ps[:, 2 * h:2 * h + 2, 0:CH], fil[:].to_broadcast([P, 2, CH]),
                                        ALU.mult).then_inc(tf_ready, 1)

            def window(S, R):
                w, w0 = S - 1, R - 1
                r = win_rows(w0)

                def first(k, op):
                    dst, src, wt = op
                    if w0 < NS:
                        dve.wait_ge(t_ready, S * (NG * KT))
                        wait(dve, halo_ready, w * KT)
                    if begins(w0) or w0 == NS:
                        wait(dve, edge_ready, w0 // STRIPS * KT)
                    wait(dve, g_ready, w * 2)
                    nc.vector.tensor_scalar(dst, src, wt, None, ALU.mult).then_inc(tap[k], 1)

                def other(k, n, op):
                    dst, src, wt = op
                    if n == 0 and w0 == NS:
                        dve.wait_ge(center_ready[k], w + firsts(w0) + 1)
                    elif n == 0:
                        dve.wait_ge(tap_in[k], w * 16 + 16)
                    wait(dve, tap[k], taps_before(k, w, w0) + n)
                    nc.vector.scalar_tensor_tensor(dst, src, wt, dst, ALU.mult, ALU.add).then_inc(tap[k], 1)

                def product(k):
                    dve.wait_ge(gelu_ready, w * 2 + (2 if k == 0 else 1))
                    if k == 0:
                        dve.wait_ge(tap[1], taps_before(1, w + 1, w0 + 1))
                        a = acc[:, acc_of(1, w0), 0:r]
                        nc.vector.tensor_tensor(a, a, acc[:, ACC0, 0:r], ALU.mult).then_inc(g_ready, 1)
                    else:
                        a = acc[P - LO:P, acc_of(2, w0), 0:r]
                        nc.vector.tensor_tensor(a, a, gelu2(w0, r), ALU.mult).then_inc(g_ready, 1)

                todo = {}
                for k in range(KT):
                    centers, _, others = dw_ops(w0, k)
                    todo[k] = []
                    if k == 0:
                        todo[k] += [lambda k=k, o=o: first(k, o) for o in centers]
                    n0 = len(todo[k])
                    todo[k] += [lambda k=k, n=n, o=o, n0=n0: other(k, n + n0, o) for n, o in enumerate(others)]
                a, b, c = (todo[k] for k in range(KT))
                la = len(a) - 3
                ops = a[:la]
                for n in range(3):
                    ops += a[la + n:la + n + 1] + c[n:n + 1]
                if len(c) > 3:
                    c = c[3:]
                    for n in range(len(c)):
                        ops += c[n:n + 1] + b[n:n + 1]
                    b = b[len(c):]
                ops += b[:2] + [lambda: product(2)] + b[2:] + [lambda: product(0)]
                return ops

            def rest(S, R):
                w, w0 = S - 2, R - 2
                r = win_rows(w0)
                dve.wait_ge(g2_ready, w * 2 + 1)
                wait(dve, w_done, w * (KT * NG))
                nc.vector.tensor_tensor(g2[0:LO, 0:r], acc[P - LO:P, acc_of(2, w0), 0:r],
                                        g2[P - LO:P, 0:r].bitcast(F32), ALU.subtract).then_inc(g2_ready, 1)

            def step(S, R):
                ops = window(S, R) if 1 <= R <= NS + 1 else []
                if R >= 2:
                    ops[1:1] = [lambda: rest(S, R)]
                for p in range(NG):
                    mine = ops[len(ops) * p // NG:len(ops) * (p + 1) // NG]
                    Sg, Rg, j = (S, R, p + 1) if p < NG - 1 else (S + 1, R + 1, 0)
                    ahead = max(len(mine) - 2, 0)
                    if R == STRIPS - 1:
                        if p == 0:
                            sums_to_stats()
                            group_stats(1, 0, None)
                        else:
                            group_stats(1, (1, 2, 4)[p - 1], 4 + (2 * p) % 4)
                    for op in mine[:ahead]:
                        op()
                    if Rg < NS:
                        stage_c(Sg, j, 0)
                    for op in mine[ahead:ahead + 1]:
                        op()
                    if Rg < NS:
                        stage_c(Sg, j, 1)
                    if p < NG - 2:
                        rest_of_x(S, R, p + 2)
                    else:
                        rest_of_x(S + 1, R + 1, p + 2 - NG)
                    if R == STRIPS - 1 and p == 2:
                        group_stats(1, 3, None)
                    for op in mine[ahead + 1:]:
                        op()

            rest_of_x(0, 0, 0)
            for h in range(2):
                stage_c(0, 0, h)
            rest_of_x(0, 0, 1)
            pipeline(dve, step)


def _constants(np):
    rows = np.arange(EDGE)
    basis, entries = [], []
    for k1 in range(EDGE):
        for k2 in range(EDGE // 2 + 1):
            angle = 2 * np.pi * (k1 * rows[:, None] + k2 * rows[None, :]) / EDGE
            k1n = (-k1) % EDGE
            own = k2 in (0, EDGE // 2)
            weight = np.zeros((EDGE, EDGE // 2 + 1))
            if own and k1 == k1n:
                weight[k1, k2] = 1.0
                basis.append(np.cos(angle) / EDGE)
                entries.append(weight)
            elif not own or k1 < k1n:
                weight[k1, k2] += 0.5 if own else 1.0
                if own:
                    weight[k1n, k2] += 0.5
                for f in (np.cos(angle), np.sin(angle)):
                    basis.append(f * np.sqrt(2.0) / EDGE)
                    entries.append(weight)
    basis = np.stack(basis)
    n = len(basis)
    dft = np.zeros((EDGE, 2, EDGE, 2, n))
    for patch in range(2):
        dft[:, patch, :, patch, :] = basis.transpose(1, 2, 0)
    dft = dft.reshape(P, P).astype(np.float32)
    entries = np.stack(entries).reshape(n, -1)
    select = np.concatenate([entries, entries]).T.astype(np.float32)
    group = np.arange(CH) // CPG
    group_mean = ((group[:, None] == group[None, :]) / CPG).astype(np.float32)
    return {"dft": dft, "dft_t": dft.T, "select": select, "group_mean": group_mean}


def kernel(x, L0_conv_fft_filter, L0_conv_w_in, L0_conv_w_dw, L0_conv_w_out):
    import numpy as np
    import concourse.bacc as bacc
    from concourse.bass_utils import run_bass_kernel_spmd as run

    order = np.concatenate([np.arange(P), HID2 + np.arange(P), np.arange(P, HID2), HID2 + np.arange(P, HID2)])
    w_in, w_dw, w_out = np.asarray(L0_conv_w_in), np.asarray(L0_conv_w_dw), np.asarray(L0_conv_w_out)
    fft = np.asarray(L0_conv_fft_filter)
    arrays = {
        "x": np.asarray(x),
        "w_in": w_in[order].T,
        "w_out": w_out.T,
        "w_dw": np.concatenate([w_dw[order].reshape(CH, 9), fft[order][:, 0, 0:1]], axis=1),
        "filt": fft[order].reshape(CH, -1).T,
        **_constants(np),
    }
    arrays = {f"in_{k}": np.ascontiguousarray(v) for k, v in arrays.items()}
    nc = bacc.Bacc("TRN2", target_bir_lowering=False, num_devices=1)
    args = [nc.dram_tensor(n, a.shape, mybir.dt.from_np(a.dtype), kind="ExternalInput").ap()
            for n, a in arrays.items()]
    out = nc.dram_tensor("out", (NB, CH, H, W), F32, kind="ExternalOutput").ap()
    conv_kernel(nc, *args, out)
    r = run(nc, [arrays], core_ids=[0])
    return r.results[0]["out"]
```
